# Optimizing a Trainium2 kernel written in Bass

```python
import numpy as np
import jax
import jax.numpy as jnp

def _softmax(x, axis=-1):
    return jax.nn.softmax(x, axis=axis)

def _gelu(x):
    return jax.nn.gelu(x, approximate=True)

def _silu(x):
    return jax.nn.silu(x)

def _sigmoid(x):
    return jax.nn.sigmoid(x)

def _layernorm(x, axis=-1, eps=1e-05):
    m = jnp.mean(x, axis=axis, keepdims=True)
    v = jnp.var(x, axis=axis, keepdims=True)
    return (x - m) / jnp.sqrt(v + eps)

def _scatter_add(tgt, idx, src, axis=0):
    return tgt.at[idx].add(src)

def _segment_sum(src, seg, n):
    return jax.ops.segment_sum(src, seg, n)
kernel_name = 'mk_recurrent_d1_jaxref_r4_187eda'

def setup_inputs(seed: int=0):
    np.random.seed(seed)
    _w = jnp.asarray

    def _L0_attn_setup():
        import jax, jax.numpy as jnp
        import numpy as np
        DIM = 512
        STATE = 64
        DT_RANK = 128
        EPS = 1e-05
        key = jax.random.key(seed)
        ks = jax.random.split(key, 8)
        B, L = (2, 1024)
        x = jax.random.normal(ks[0], (B, L, DIM), dtype=jnp.float32)
        norm_w = jnp.ones((DIM,), jnp.float32)
        norm_b = jnp.zeros((DIM,), jnp.float32)
        x_proj_w = jax.random.normal(ks[1], (DT_RANK + 2 * STATE, DIM), jnp.float32) / np.sqrt(DIM)
        dt_proj_w = jax.random.normal(ks[2], (DIM, DT_RANK), jnp.float32) / np.sqrt(DT_RANK)
        dt_proj_b = jax.random.normal(ks[3], (DIM,), jnp.float32) * 0.1
        A_log = jnp.log(jnp.broadcast_to(jnp.arange(1, STATE + 1, dtype=jnp.float32), (DIM, STATE)))
        D_param = jnp.ones((DIM,), jnp.float32)
        out_proj_w = jax.random.normal(ks[4], (DIM, DIM), jnp.float32) / np.sqrt(DIM)
        return {'x': x, 'norm_w': norm_w, 'norm_b': norm_b, 'x_proj_w': x_proj_w, 'dt_proj_w': dt_proj_w, 'dt_proj_b': dt_proj_b, 'A_log': A_log, 'D_param': D_param, 'out_proj_w': out_proj_w}
    _L0_attn_in = _L0_attn_setup()

    def _L0_ffn_setup():
        import jax, jax.numpy as jnp
        import numpy as np
        B, S, D, F, E, SH, K = (2, 512, 512, 256, 16, 2, 2)

        def _experts_all(x, g, gb, w1, b1, w2, b2):
            y = jax.nn.gelu(jnp.einsum('bsd,edf->bsef', x, g) + gb, approximate=False)
            y = y * (jnp.einsum('bsd,edf->bsef', x, w1) + b1)
            return jnp.einsum('bsef,efd->bsed', y, w2) + b2
        key = jax.random.key(seed)
        ks = jax.random.split(key, 8)
        std = 0.02
        mk = lambda k, sh: jax.random.normal(k, sh, jnp.float32) * std
        return {'x': jax.random.normal(ks[0], (B, S, D), jnp.float32), 'wa': mk(ks[1], (D, E)), 'rg': mk(ks[2], (E, D, F)), 'rgb': jnp.zeros((E, F), jnp.float32), 'rw1': mk(ks[3], (E, D, F)), 'rb1': jnp.zeros((E, F), jnp.float32), 'rw2': mk(ks[4], (E, F, D)), 'rb2': jnp.zeros((E, D), jnp.float32), 'sg': mk(ks[5], (SH, D, F)), 'sgb': jnp.zeros((SH, F), jnp.float32), 'sw1': mk(ks[6], (SH, D, F)), 'sb1': jnp.zeros((SH, F), jnp.float32), 'sw2': mk(ks[7], (SH, F, D)), 'sb2': jnp.zeros((SH, D), jnp.float32)}
    _L0_ffn_in = _L0_ffn_setup()
    _d = {'L0_attn_x': _L0_attn_in['x'], 'L0_attn_norm_w': _L0_attn_in['norm_w'], 'L0_attn_norm_b': _L0_attn_in['norm_b'], 'L0_attn_x_proj_w': _L0_attn_in['x_proj_w'], 'L0_attn_dt_proj_w': _L0_attn_in['dt_proj_w'], 'L0_attn_dt_proj_b': _L0_attn_in['dt_proj_b'], 'L0_attn_A_log': _L0_attn_in['A_log'], 'L0_attn_D_param': _L0_attn_in['D_param'], 'L0_attn_out_proj_w': _L0_attn_in['out_proj_w'], 'L0_ffn_wa': _L0_ffn_in['wa'], 'L0_ffn_rg': _L0_ffn_in['rg'], 'L0_ffn_rgb': _L0_ffn_in['rgb'], 'L0_ffn_rw1': _L0_ffn_in['rw1'], 'L0_ffn_rb1': _L0_ffn_in['rb1'], 'L0_ffn_rw2': _L0_ffn_in['rw2'], 'L0_ffn_rb2': _L0_ffn_in['rb2'], 'L0_ffn_sg': _L0_ffn_in['sg'], 'L0_ffn_sgb': _L0_ffn_in['sgb'], 'L0_ffn_sw1': _L0_ffn_in['sw1'], 'L0_ffn_sb1': _L0_ffn_in['sb1'], 'L0_ffn_sw2': _L0_ffn_in['sw2'], 'L0_ffn_sb2': _L0_ffn_in['sb2']}
    _x0 = _d['L0_attn_x']
    _d['L0_attn_x'] = jax.random.normal(jax.random.fold_in(jax.random.key(seed), 1), (2, 2048, 512), dtype=_x0.dtype)
    del _x0
    return _d

def reference(L0_attn_x, L0_attn_norm_w, L0_attn_norm_b, L0_attn_x_proj_w, L0_attn_dt_proj_w, L0_attn_dt_proj_b, L0_attn_A_log, L0_attn_D_param, L0_attn_out_proj_w, L0_ffn_wa, L0_ffn_rg, L0_ffn_rgb, L0_ffn_rw1, L0_ffn_rb1, L0_ffn_rw2, L0_ffn_rb2, L0_ffn_sg, L0_ffn_sgb, L0_ffn_sw1, L0_ffn_sb1, L0_ffn_sw2, L0_ffn_sb2):

    def _L0_attn_ref(x, norm_w, norm_b, x_proj_w, dt_proj_w, dt_proj_b, A_log, D_param, out_proj_w):
        import jax, jax.numpy as jnp
        import numpy as np
        DIM = 512
        STATE = 64
        DT_RANK = 128
        EPS = 1e-05
        B, L, D = x.shape
        mu = jnp.mean(x, axis=-1, keepdims=True)
        var = jnp.mean(jnp.square(x - mu), axis=-1, keepdims=True)
        xn = (x - mu) * jax.lax.rsqrt(var + EPS) * norm_w + norm_b
        proj = jnp.einsum('bld,pd->blp', xn, x_proj_w)
        delta_r = proj[..., :DT_RANK]
        B_ssm = proj[..., DT_RANK:DT_RANK + STATE]
        C_ssm = proj[..., DT_RANK + STATE:]
        delta = jax.nn.softplus(jnp.einsum('blr,dr->bld', delta_r, dt_proj_w) + dt_proj_b)
        A = -jnp.exp(A_log)

        def step(h, inp):
            dt, b, xt, c = inp
            dA = jnp.exp(dt[..., None] * A)
            h = dA * h + dt[..., None] * b[:, None, :] * xt[..., None]
            y = jnp.einsum('bdn,bn->bd', h, c)
            return (h, y)
        h0 = jnp.zeros((B, D, STATE), x.dtype)
        xs = (jnp.swapaxes(delta, 0, 1), jnp.swapaxes(B_ssm, 0, 1), jnp.swapaxes(xn, 0, 1), jnp.swapaxes(C_ssm, 0, 1))
        _, ys = jax.lax.scan(step, h0, xs)
        y = jnp.swapaxes(ys, 0, 1)
        return jnp.einsum('bld,od->blo', y + x * D_param, out_proj_w)

    def _L0_ffn_ref(x, wa, rg, rgb, rw1, rb1, rw2, rb2, sg, sgb, sw1, sb1, sw2, sb2):
        import jax, jax.numpy as jnp
        import numpy as np
        B, S, D, F, E, SH, K = (2, 512, 512, 256, 16, 2, 2)

        def _experts_all(x, g, gb, w1, b1, w2, b2):
            y = jax.nn.gelu(jnp.einsum('bsd,edf->bsef', x, g) + gb, approximate=False)
            y = y * (jnp.einsum('bsd,edf->bsef', x, w1) + b1)
            return jnp.einsum('bsef,efd->bsed', y, w2) + b2
        aff = jax.nn.sigmoid(jnp.einsum('bsd,de->bse', x, wa))
        topk_p, topk_i = jax.lax.top_k(aff, K)
        topk_p = topk_p / jnp.sum(topk_p, axis=-1, keepdims=True)
        combine = jnp.sum(jax.nn.one_hot(topk_i, E, dtype=x.dtype) * topk_p[..., None], axis=2)
        routed = jnp.einsum('bsed,bse->bsd', _experts_all(x, rg, rgb, rw1, rb1, rw2, rb2), combine)
        shared = jnp.sum(_experts_all(x, sg, sgb, sw1, sb1, sw2, sb2), axis=2)
        return x + shared + routed
    x = L0_attn_x
    xn = _layernorm(x, axis=-1)
    s = _L0_attn_ref(xn, L0_attn_norm_w, L0_attn_norm_b, L0_attn_x_proj_w, L0_attn_dt_proj_w, L0_attn_dt_proj_b, L0_attn_A_log, L0_attn_D_param, L0_attn_out_proj_w)
    g = _silu(_L0_ffn_ref(xn, L0_ffn_wa, L0_ffn_rg, L0_ffn_rgb, L0_ffn_rw1, L0_ffn_rb1, L0_ffn_rw2, L0_ffn_rb2, L0_ffn_sg, L0_ffn_sgb, L0_ffn_sw1, L0_ffn_sb1, L0_ffn_sw2, L0_ffn_sb2))
    x = x + s * g
    return x

_drawn_inputs = setup_inputs


def setup_inputs(seed=0):
    import zlib

    import numpy as np

    out = dict(_drawn_inputs(seed))
    spreads = {'L0_attn_norm_w': (1.0, 0.2),
     'L0_attn_norm_b': (0.0, 0.1),
     'L0_attn_D_param': (1.0, 0.6),
     'L0_ffn_rgb': (0.0, 0.8),
     'L0_ffn_rb1': (0.0, 0.8),
     'L0_ffn_rb2': (0.0, 0.1),
     'L0_ffn_sgb': (0.0, 0.662),
     'L0_ffn_sb1': (0.0, 0.649),
     'L0_ffn_sb2': (0.0, 0.1)}
    factors = {}
    for name, (base, spread) in spreads.items():
        noise = np.random.default_rng([zlib.crc32(name.encode()), seed]).standard_normal(out[name].shape)
        drawn = base * np.exp(spread * noise) if base else spread * noise
        out[name] = jnp.asarray(drawn.astype(out[name].dtype))
    for name, factor in factors.items():
        out[name] = (out[name] * factor).astype(out[name].dtype)
    return out
```

```python
from contextlib import ExitStack

import concourse.bass as bass
from concourse import mybir

F32 = mybir.dt.float32
U32 = mybir.dt.uint32
ALU = mybir.AluOpType
ACT = mybir.ActivationFunctionType

P = 128
DIM = 512
G = DIM // P
T = 512
TS = T // P
BATCH, SEQ = 2, 2048
CPB = SEQ // T
CHUNKS = BATCH * CPB
NS = 64
RANK = 128
E, SH, F = 16, 2, 256
ITEMS = E + SH
FT = F // P
NPE = NS // E
EPS = 1e-5
UNITS = NS * G
HEAD = 4

SLOTS = {0: ("gate", 0, 0), 1: ("gate", 0, 1), 2: ("gate", 1, 0), 3: ("gate", 1, 1),
         6: ("up", 0, 0), 7: ("up", 0, 1), 8: ("up", 1, 0), 9: ("up", 1, 1),
         12: ("down", 0, 0), 13: ("down", 1, 0), 14: ("down", 2, 0), 15: ("down", 3, 0)}
DVE_LINKS = 32


def build(nc, x, xpw, dtw, wa, ow, cols, a_log, ew, eb, eb2, eye, iota, out):
    x_v = x.rearrange("(c s p) d -> c p s d", s=TS, p=P)
    out_v = out.rearrange("(c s p) d -> c p s d", s=TS, p=P)
    bt_dram = nc.dram_tensor("bt_scratch", [CHUNKS, NS, T], F32, kind="Internal").ap()

    with ExitStack() as ctx:
        def sb(name, shape, dt=F32):
            return ctx.enter_context(nc.sbuf_tensor(name, shape, dt))

        def sem(name):
            return ctx.enter_context(nc.semaphore(name))

        xpw_sb = sb("xpw_sb", [P, G, RANK + 2 * NS])
        dtw_sb = sb("dtw_sb", [P, DIM])
        wa_sb = sb("wa_sb", [P, G, E])
        ow_sb = sb("ow_sb", [P, G, DIM])
        cols_sb = sb("cols_sb", [P, 4, G])
        nw, nb, dtb, dpar = (cols_sb[:, i, :] for i in range(4))
        A = sb("A", [P, G, NS])
        eb_sb = sb("eb_sb", [P, 2, ITEMS, FT])
        eb2_sb = sb("eb2_sb", [ITEMS, DIM])
        eye_sb = sb("eye_sb", [P, P])
        iota_sb = sb("iota_sb", [P, E])
        nhalf = sb("nhalf", [P, TS])
        wg = sb("wg", [P, G, F])
        wu = sb("wu", [P, G, F])
        wd = sb("wd", [P, FT, DIM])
        xt = sb("xt", [P, TS, DIM])
        xn0 = sb("xn0", [P, TS, DIM])
        xh1 = sb("xh1", [P, TS, DIM])
        x0T = sb("x0T", [P, G, T])
        xnT = sb("xnT", [P, G, T])
        stats = sb("stats", [P, TS, 6])
        mv = sb("mv", [P, TS, 2])
        veps = sb("veps", [P, TS])
        rstd = sb("rstd", [P, TS])
        drT = sb("drT", [P, T])
        bT = sb("bT", [NS, T])
        cc = sb("cc", [P, TS, NS])
        sp = sb("sp", [P, G, T])
        spl = sb("spl", [P, G, T])
        aff = sb("aff", [P, TS, E])
        m8 = sb("m8", [P, TS, 8])
        i8 = sb("i8", [P, TS, 8], U32)
        i8f = sb("i8f", [P, TS, 8])
        psum2 = sb("psum2", [P, TS])
        pw = sb("pw", [P, TS, 2])
        W1 = sb("W1", [P, TS, E])
        W2 = sb("W2", [P, TS, E])
        W = sb("W", [P, TS, ITEMS])
        WT = sb("WT", [ITEMS, T])
        facc = sb("facc", [P, TS, DIM])
        yacc = sb("yacc", [P, TS, DIM])
        state = sb("state", [P, G, NS])
        h = sb("h", [P, 2, G, T])
        dbx = sb("dbx", [P, G, T])
        bbc = sb("bbc", [P, NPE, T])
        hg = sb("hg", [P, FT, T])
        hid = sb("hid", [P, FT, T])

        hT = [ctx.enter_context(nc.psum_tensor(f"hT{i}", [P, 512], F32)) for i in range(TS)]
        dA = [ctx.enter_context(nc.psum_tensor(f"dA{i}", [P, 512], F32)) for i in range(2)]
        FP = [ctx.enter_context(nc.psum_tensor(f"FP{i}", [P, 512], F32)) for i in range(2)]
        pre_bank = [dA[0], dA[1], FP[0], FP[1]]

        const_in = sem("const_in")
        x_in = sem("x_in")
        bt_out = sem("bt_out")
        b_in = [sem(f"b_in{i}") for i in range(NPE)]
        wg_in, wu_in, wd_in = sem("wg_in"), sem("wu_in"), sem("wd_in")
        out_dma = sem("out_dma")
        a_exp = sem("a_exp")
        dve_const = sem("dve_const")
        dve_link = sem("dve_link")
        stats_done = sem("stats_done")
        rstd_add = sem("rstd_add")
        rstd_done = sem("rstd_done")
        norm_done = sem("norm_done")
        tr_done = sem("tr_done")
        trc_done = sem("trc_done")
        proj_done = sem("proj_done")
        projc_done = sem("projc_done")
        cc_done = sem("cc_done")
        pre_done = sem("pre_done")
        abs_done = sem("abs_done")
        relu_done = sem("relu_done")
        spe_done = sem("spe_done")
        ln_done = sem("ln_done")
        delta_done = sem("delta_done")
        u_done = sem("u_done")
        rexp_done = sem("rexp_done")
        w_done = sem("w_done")
        wt_done = sem("wt_done")
        wtc_done = sem("wtc_done")
        bias_done = sem("bias_done")
        facc_done = sem("facc_done")
        exp_done = sem("exp_done")
        dbx_done = sem("dbx_done")
        scan_done = sem("scan_done")
        hT_done = sem("hT_done")
        y_done = sem("y_done")
        state_done = sem("state_done")
        ffn_done = sem("ffn_done")
        gelu_done = sem("gelu_done")
        hid_done = sem("hid_done")
        comb_done = sem("comb_done")
        yT_done = sem("yT_done")
        z_done = sem("z_done")
        s_done = sem("s_done")
        sexp_done = sem("sexp_done")
        sig_done = sem("sig_done")
        fin_done = sem("fin_done")

        passed = sem("passed")

        FFN = 2 * FT + TS

        block = ctx.enter_context(nc.Block())

        def wait_alone(eng, sem, value):
            eng.wait_ge(sem, value)
            eng.sem_inc(passed, 1)

        @block.sync
        def _(sp):
            for dst, src in ((xpw_sb, xpw), (dtw_sb, dtw), (wa_sb, wa), (ow_sb, ow), (cols_sb, cols), (A, a_log),
                             (eb_sb, eb), (eb2_sb, eb2), (eye_sb, eye), (iota_sb, iota)):
                sp.dma_start(dst[:], src).then_inc(const_in, 16)

            def load_gate(c, i, first=False):
                if not first:
                    sp.wait_ge(ffn_done, (c * ITEMS + i) * FFN - FFN + FT + HEAD)
                sp.dma_start(wg[:], ew[i, :, 0:G * F].rearrange("p (k f) -> p k f", k=G)).then_inc(wg_in, 16)

            def load_up(c, i, first=False):
                if not first:
                    sp.wait_ge(ffn_done, (c * ITEMS + i) * FFN - FFN + 2 * FT + HEAD)
                sp.dma_start(wu[:], ew[i, :, G * F:2 * G * F].rearrange("p (k f) -> p k f", k=G)).then_inc(wu_in, 16)

            def load_down(c, i, first=False):
                if not first:
                    sp.wait_ge(ffn_done, (c * ITEMS + i) * FFN + HEAD)
                sp.dma_start(wd[:], ew[i, :, 2 * G * F:].rearrange("p (k d) -> p k d", k=FT)).then_inc(wd_in, 16)

            def load_b(c, n, j):
                sp.dma_start(bbc[:, j, :], bt_dram[c, n, :].partition_broadcast(P)).then_inc(b_in[j], 16)

            with sp.Fori(0, CHUNKS) as c:
                sp.wait_ge(fin_done, c * TS + HEAD)
                sp.dma_start(xt[:], x_v[c]).then_inc(x_in, 16)
                sp.wait_ge(ffn_done, c * (ITEMS * FFN) + HEAD)
                load_gate(c, 0, True)
                load_up(c, 0, True)
                load_down(c, 0, True)
                sp.wait_ge(projc_done, c * 2 + 2)
                sp.dma_start(bt_dram[c], bT[:]).then_inc(bt_out, 16)
                sp.wait_ge(bt_out, c * 16 + 16)
                for j in range(NPE):
                    load_b(c, j, j)

                def body(e, last=False):
                    for k in range(NPE):
                        if not last:
                            sp.wait_ge(dbx_done, c * UNITS + e * (NPE * G) + (k + 1) * G)
                            load_b(c, e * NPE + NPE + k, k)
                        if k == 1:
                            load_gate(c, e + 1)
                        if k == 2:
                            load_up(c, e + 1)
                    load_down(c, e + 1)

                with sp.Fori(0, E - 1) as e:
                    body(e)
                body(E - 1, True)
                for s in range(E + 1, ITEMS):
                    load_gate(c, s)
                    load_up(c, s)
                    load_down(c, s)
                sp.wait_ge(fin_done, c * TS + TS + HEAD)
                sp.dma_start(out_v[c], xh1[:]).then_inc(out_dma, 16)
                wait_alone(sp, out_dma, c * 16 + 16)

        @block.gpsimd
        def _(pool):
            pool.wait_ge(dve_const, 2)
            with pool.Fori(0, CHUNKS) as c:
                for r in range(2):
                    wait_alone(pool, stats_done, c * 2 + r + 1)
                    pool.tensor_scalar(veps[:], mv[:, :, 1], EPS, None, ALU.add).then_inc(rstd_add, 1)
                    pool.wait_ge(rstd_add, c * 2 + r + 1)
                    pool.tensor_tensor(rstd[:], veps[:], nhalf[:], ALU.pow).then_inc(rstd_done, 1)
                wait_alone(pool, u_done, c + 1)
                with pool.Fori(0, E) as e:
                    for k in range(NPE):
                        pool.wait_ge(b_in[k], c * (E * 16) + e * 16 + 16)
                        for g in range(G):
                            pool.wait_ge(scan_done, c * UNITS + e * (NPE * G) + (k * G + g - G + 1) + HEAD)
                            pool.tensor_tensor(dbx[:, g, :], spl[:, g, :], bbc[:, k, :], ALU.mult)\
                                .then_inc(dbx_done, 1)

        @block.scalar
        def _(act):
            act.wait_ge(const_in, 160)
            act.activation(A[:], A[:], ACT.Exp).then_inc(a_exp, 1)
            act.wait_ge(dve_const, 3)
            with act.Fori(0, CHUNKS) as c:
                for g in range(G):
                    act.wait_ge(tr_done, c * (2 * G) + g + 1)
                    act.activation(x0T[:, g, :], hT[g][:], ACT.Copy).then_inc(trc_done, 1)
                for g in range(G):
                    act.wait_ge(tr_done, c * (2 * G) + G + g + 1)
                    act.activation(xnT[:, g, :], pre_bank[g][:], ACT.Identity, scale=nw[:, g:g + 1],
                                   bias=nb[:, g:g + 1]).then_inc(trc_done, 1)
                act.wait_ge(proj_done, c * 4 + 1)
                act.activation(drT[:], hT[0][:], ACT.Copy).then_inc(projc_done, 1)
                act.wait_ge(proj_done, c * 4 + 2)
                act.activation(bT[:], hT[1][0:NS, :], ACT.Copy).then_inc(projc_done, 1)
                for g in range(G):
                    act.wait_ge(pre_done, c * G + g + 1)
                    act.activation(spl[:, g, :], pre_bank[g][:], ACT.Abs, bias=dtb[:, g:g + 1]).then_inc(abs_done, 1)
                act.wait_ge(abs_done, c * G + G)
                act.activation(spl[:], spl[:], ACT.Exp, scale=-1.0).then_inc(spe_done, 1)
                act.wait_ge(spe_done, c + 1)
                act.activation(spl[:], spl[:], ACT.Ln, bias=1.0).then_inc(ln_done, 1)
                act.wait_ge(proj_done, c * 4 + 4)
                act.activation(aff[:], hT[3][:, 0:TS * E].rearrange("p (s e) -> p s e", s=TS), ACT.Exp,
                               scale=-1.0).then_inc(rexp_done, 1)
                act.wait_ge(wt_done, c + 1)
                act.activation(WT[:], dA[0][0:ITEMS, :], ACT.Copy).then_inc(wtc_done, 1)
                act.wait_ge(delta_done, c + 1)
                act.wait_ge(wtc_done, c + 1)

                def gelu(i, f):
                    act.wait_ge(ffn_done, c * (ITEMS * FFN) + i * FFN + f + 1 + HEAD)
                    act.activation(hg[:, f, :], FP[f][:], ACT.Gelu, bias=eb_sb[:, 0, bass.ds(i, 1), f])\
                        .then_inc(gelu_done, 1)

                with act.Fori(0, E) as e:
                    for k in range(NPE):
                        for g in range(G):
                            act.wait_ge(scan_done, c * UNITS + e * (NPE * G) + (k * G + g - 1) + HEAD)
                            act.activation(dA[g % 2][:], sp[:, g, :], ACT.Exp, scale=A[:, g, bass.ds(e * NPE + k, 1)])\
                                .then_inc(exp_done, 1)
                            if (k, g) == (2, 1):
                                for f in range(FT):
                                    gelu(e, f)
                for s in range(E, ITEMS):
                    for f in range(FT):
                        gelu(s, f)
                act.wait_ge(comb_done, (c + 1) * (ITEMS * TS) + HEAD)
                act.activation(xh1[:], facc[:], ACT.Exp, scale=-1.0).then_inc(sexp_done, 1)

        @block.vector
        def _(dve):
            dve.memset(nhalf[:], -0.5).then_inc(dve_const, 1)
            dve.memset(W[:], 1.0).then_inc(dve_const, 1)
            for done in (scan_done, comb_done, fin_done):
                dve.sem_inc(done, HEAD)
            dve.wait_ge(a_exp, 1)
            dve.tensor_scalar(A[:], A[:], -1.0, None, ALU.mult).then_inc(dve_const, 1)
            dve.wait_ge(dve_const, 3)

            with dve.Fori(0, BATCH) as b:
                dve.memset(state[:], 0.0)
                with dve.Fori(0, CPB) as cb:
                    c = b * CPB + cb
                    links = [0]

                    def link(ins):
                        links[0] += 1
                        ins.then_inc(dve_link, 1)
                        wait_alone(dve, dve_link, c * DVE_LINKS + links[0])

                    wait_alone(dve, x_in, c * 16 + 16)
                    for r, (src, dst) in enumerate(((xt, xn0), (xn0, xh1))):
                        for s in range(TS):
                            last = dve.bn_stats(stats[:, s, :], src[:, s, :])
                        link(last)
                        for s in range(TS):
                            last = dve.bn_aggr(mv[:, s, :], stats[:, s, :])
                        last.then_inc(stats_done, 1)
                        dve.wait_ge(rstd_done, c * 2 + r + 1)
                        for s in range(TS):
                            last = dve.tensor_scalar(dst[:, s, :], src[:, s, :], mv[:, s, 0:1], rstd[:, s:s + 1],
                                                     ALU.subtract, ALU.mult)
                        last.then_inc(norm_done, 1)
                        wait_alone(dve, norm_done, c * 2 + r + 1)
                    dve.wait_ge(proj_done, c * 4 + 3)
                    dve.tensor_copy(cc[:], hT[2][:, 0:TS * NS].rearrange("p (s n) -> p s n", s=TS)).then_inc(cc_done, 1)
                    for g in range(G):
                        dve.wait_ge(abs_done, c * G + g + 1)
                        dve.tensor_scalar(sp[:, g, :], pre_bank[g][:], dtb[:, g:g + 1], 0.0, ALU.add, ALU.max)\
                            .then_inc(relu_done, 1)
                    dve.wait_ge(relu_done, c * G + G)
                    dve.wait_ge(ln_done, c + 1)
                    dve.tensor_tensor(sp[:], sp[:], spl[:], ALU.add).then_inc(delta_done, 1)
                    dve.wait_ge(delta_done, c + 1)
                    dve.tensor_tensor(spl[:], sp[:], xnT[:], ALU.mult).then_inc(u_done, 1)

                    dve.wait_ge(rexp_done, c + 1)
                    link(dve.tensor_scalar(aff[:], aff[:], 1.0, None, ALU.add))
                    link(dve.reciprocal(aff[:], aff[:]))
                    for s in range(TS):
                        last = dve.max(m8[:, s, :], aff[:, s, :])
                    link(last)
                    for s in range(TS):
                        last = dve.max_index(i8[:, s, :], m8[:, s, :], aff[:, s, :])
                    link(last)
                    link(dve.tensor_copy(i8f[:], i8[:]))
                    link(dve.tensor_tensor(psum2[:], m8[:, :, 0], m8[:, :, 1], ALU.add))
                    link(dve.reciprocal(psum2[:], psum2[:]))
                    for j in range(2):
                        last = dve.tensor_tensor(pw[:, :, j], m8[:, :, j], psum2[:], ALU.mult)
                    link(last)
                    for s in range(TS):
                        for j, w in enumerate((W1, W2)):
                            last = dve.tensor_scalar(w[:, s, :], iota_sb[:], i8f[:, s, j:j + 1], pw[:, s, j:j + 1],
                                                     ALU.is_equal, ALU.mult)
                    link(last)
                    dve.tensor_tensor(W[:, :, 0:E], W1[:], W2[:], ALU.add).then_inc(w_done, 1)
                    for s in range(TS):
                        dve.wait_ge(bias_done, c * TS + s + 1)
                        dve.tensor_tensor(facc[:, s, :], hT[s][:], xn0[:, s, :], ALU.add).then_inc(facc_done, 1)
                    dve.wait_ge(facc_done, c * TS + TS)

                    def scan(n, k, g):
                        unit = n * G + g
                        dve.wait_ge(exp_done, c * UNITS + unit + 1)
                        dve.wait_ge(dbx_done, c * UNITS + unit + 1)
                        dve.tensor_tensor_scan(h[:, k % 2, g, :], dA[g % 2][:], dbx[:, g, :],
                                               state[:, g, bass.ds(n, 1)], ALU.mult, ALU.add).then_inc(scan_done, 1)

                    def y_add(n, s, first=False):
                        dve.wait_ge(hT_done, c * (NS * TS) + n * TS + s + 1)
                        if first:
                            dve.tensor_scalar(yacc[:, s, :], hT[s][:], cc[:, s, bass.ds(n, 1)], None,
                                              ALU.mult).then_inc(y_done, 1)
                            return
                        dve.wait_ge(y_done, c * (NS * TS) + n * TS + s + 1 - TS)
                        dve.scalar_tensor_tensor(yacc[:, s, :], hT[s][:], cc[:, s, bass.ds(n, 1)], yacc[:, s, :],
                                                 ALU.mult, ALU.add).then_inc(y_done, 1)

                    def keep_state(n, k):
                        wait_alone(dve, scan_done, c * UNITS + n * G + G + HEAD)
                        dve.tensor_copy(state[:, :, bass.ds(n, 1)], h[:, k % 2, :, T - 1:T]).then_inc(state_done, 1)

                    def hidden(i, f):
                        dve.wait_ge(ffn_done, c * (ITEMS * FFN) + i * FFN + FT + f + 1 + HEAD)
                        dve.wait_ge(gelu_done, c * (ITEMS * FT) + i * FT + f + 1)
                        dve.scalar_tensor_tensor(hid[:, f, :], FP[f][:], eb_sb[:, 1, bass.ds(i, 1), f], hg[:, f, :],
                                                 ALU.add, ALU.mult).then_inc(hid_done, 1)

                    def combine(i, s):
                        dve.wait_ge(ffn_done, c * (ITEMS * FFN) + i * FFN + 2 * FT + s + 1 + HEAD)
                        dve.scalar_tensor_tensor(facc[:, s, :], FP[s % 2][:], W[:, s, bass.ds(i, 1)], facc[:, s, :],
                                                 ALU.mult, ALU.add).then_inc(comb_done, 1)

                    def step(n, k, first=None, item=None, lag=None):
                        scan(n, k, 0)
                        scan(n, k, 1)
                        if lag != "none":
                            y_add(n - 1, 0, lag == "first")
                        scan(n, k, 2)
                        if lag != "none":
                            y_add(n - 1, 1, lag == "first")
                        if item is not None and k == 0:
                            combine(item, 0)
                            combine(item, 1)
                        scan(n, k, 3)
                        if item is not None and k == 3:
                            hidden(item, 0)
                        if lag != "none":
                            y_add(n - 1, 2, lag == "first")
                            y_add(n - 1, 3, lag == "first")
                        if item is not None and k == 3:
                            hidden(item, 1)
                        if item is not None and k == 0:
                            combine(item, 2)
                            combine(item, 3)
                        keep_state(n, k)

                    step(0, 0, lag="none")
                    step(1, 1, lag="first")
                    step(2, 2)
                    step(3, 3, item=0)
                    step(4, 0, item=0)
                    with dve.Fori(1, E - 1) as i:
                        step(i * NPE + 1, 1)
                        step(i * NPE + 2, 2)
                        step(i * NPE + 3, 3, item=i)
                        step(i * NPE + 4, 0, item=i)
                    step(NS - 3, 1)
                    step(NS - 2, 2)
                    step(NS - 1, 3, item=E - 1)
                    for s in (0, 2):
                        y_add(NS - 1, s)
                        y_add(NS - 1, s + 1)
                        combine(E - 1, s)
                        combine(E - 1, s + 1)
                    for i in range(E, ITEMS):
                        for f in range(FT):
                            hidden(i, f)
                        for s in range(TS):
                            combine(i, s)

                    for g in range(G):
                        dve.wait_ge(yT_done, c * G + g + 1)
                        dve.scalar_tensor_tensor(xnT[:, g, :], x0T[:, g, :], dpar[:, g:g + 1], hT[g][:],
                                                 ALU.mult, ALU.add).then_inc(z_done, 1)
                    dve.wait_ge(sexp_done, c + 1)
                    link(dve.tensor_scalar(xh1[:], xh1[:], 1.0, None, ALU.add))
                    link(dve.reciprocal(xh1[:], xh1[:]))
                    link(dve.tensor_tensor(xh1[:], xh1[:], facc[:], ALU.mult))
                    for s in range(TS):
                        dve.wait_ge(s_done, c * TS + s + 1)
                        link(dve.tensor_tensor(xh1[:, s, :], pre_bank[s][:], xh1[:, s, :], ALU.mult))
                        dve.tensor_tensor(xh1[:, s, :], xh1[:, s, :], xt[:, s, :], ALU.add).then_inc(fin_done, 1)
                    while links[0] < DVE_LINKS:
                        links[0] += 1
                        dve.sem_inc(dve_link, 1)
                    assert links[0] == DVE_LINKS

        @block.tensor
        def _(pe):
            pe.wait_ge(const_in, 160)
            pe.sem_inc(ffn_done, HEAD)
            with pe.Fori(0, CHUNKS) as c:
                for r, (src, banks) in enumerate(((xn0, hT), (xh1, pre_bank))):
                    pe.wait_ge(norm_done, c * 2 + r + 1)
                    for g in range(G):
                        for s in range(TS):
                            last = pe.transpose(banks[g][:, s * P:(s + 1) * P], src[:, s, g * P:(g + 1) * P], eye_sb[:])
                        last.then_inc(tr_done, 1)
                pe.wait_ge(trc_done, c * (2 * G) + 2 * G)
                for k in range(G):
                    last = pe.matmul(hT[0][:], xpw_sb[:, k, 0:RANK], xnT[:, k, :], start=(k == 0), stop=(k == G - 1))
                last.then_inc(proj_done, 1)
                for k in range(G):
                    last = pe.matmul(hT[1][0:NS, :], xpw_sb[:, k, RANK:RANK + NS], xnT[:, k, :], start=(k == 0),
                                     stop=(k == G - 1))
                last.then_inc(proj_done, 1)
                for s in range(TS):
                    for k in range(G):
                        last = pe.matmul(hT[2][:, s * NS:(s + 1) * NS], xnT[:, k, s * P:(s + 1) * P],
                                         xpw_sb[:, k, RANK + NS:], start=(k == 0), stop=(k == G - 1))
                last.then_inc(proj_done, 1)
                for s in range(TS):
                    for k in range(G):
                        last = pe.matmul(hT[3][:, s * E:(s + 1) * E], x0T[:, k, s * P:(s + 1) * P], wa_sb[:, k, :],
                                         start=(k == 0), stop=(k == G - 1))
                last.then_inc(proj_done, 1)
                pe.wait_ge(projc_done, c * 2 + 1)
                for g in range(G):
                    pe.matmul(pre_bank[g][:], dtw_sb[:, g * P:(g + 1) * P], drT[:], start=True, stop=True)\
                        .then_inc(pre_done, 1)
                pe.wait_ge(w_done, c + 1)
                pe.wait_ge(abs_done, c * G + 1)
                pe.wait_ge(relu_done, c * G + 1)
                for s in range(TS):
                    last = pe.transpose(dA[0][0:ITEMS, s * P:(s + 1) * P], W[:, s, :], eye_sb[:])
                last.then_inc(wt_done, 1)
                pe.wait_ge(wtc_done, c + 1)
                pe.wait_ge(cc_done, c + 1)
                for s in range(TS):
                    pe.matmul(hT[s][:], WT[:, s * P:(s + 1) * P], eb2_sb[:], start=True, stop=True)\
                        .then_inc(bias_done, 1)
                pe.wait_ge(facc_done, c * TS + TS)
                pe.wait_ge(relu_done, c * G + G)

                def ffn(i, kind, j, half=None):
                    base = c * (ITEMS * FFN) + i * FFN
                    bank = FP[j % 2]
                    ks = range(G) if kind != "down" else range(FT)
                    if half is not None and kind != "down":
                        ks = range(half * G // 2, (half + 1) * G // 2)
                    if ks[0] == 0:
                        if kind == "gate":
                            if j == 0:
                                pe.wait_ge(wg_in, c * (ITEMS * 16) + i * 16 + 16)
                            pe.wait_ge(comb_done, c * (ITEMS * TS) + HEAD + (0 if type(i) is int and i == 0 else i * TS - FT + j + 1))
                        elif kind == "up":
                            if j == 0:
                                pe.wait_ge(wu_in, c * (ITEMS * 16) + i * 16 + 16)
                            pe.wait_ge(gelu_done, c * (ITEMS * FT) + i * FT + j + 1)
                        elif j == 0:
                            pe.wait_ge(wd_in, c * (ITEMS * 16) + i * 16 + 16)
                            pe.wait_ge(hid_done, c * (ITEMS * FT) + i * FT + FT)
                        elif j >= 2:
                            pe.wait_ge(comb_done, c * (ITEMS * TS) + i * TS + j - 1 + HEAD)
                    for q in ks:
                        if kind == "down":
                            last = pe.matmul(bank[:], hid[:, q, j * P:(j + 1) * P], wd[:, q, :],
                                             start=(q == 0), stop=(q == FT - 1))
                        else:
                            w = wg if kind == "gate" else wu
                            last = pe.matmul(bank[:], w[:, q, j * P:(j + 1) * P], x0T[:, q, :],
                                             start=(q == 0), stop=(q == G - 1))
                    if kind == "down" or ks[-1] == G - 1:
                        last.then_inc(ffn_done, 1)

                def body(e, first=False):
                    for k in range(NPE):
                        pe.wait_ge(scan_done, c * UNITS + e * (NPE * G) + (k * G + G + HEAD))
                        for s in range(TS):
                            if not (first and k == 0):
                                pe.wait_ge(y_done, c * (NS * TS) + e * (NPE * TS) + (k * TS + s + 1 - TS))
                            for g in range(G):
                                last = pe.transpose(hT[s][:, g * P:(g + 1) * P], h[:, k % 2, g, s * P:(s + 1) * P],
                                                    eye_sb[:])
                            last.then_inc(hT_done, 1)
                            if k * TS + s in SLOTS:
                                ffn(e, *SLOTS[k * TS + s])

                body(0, True)
                with pe.Fori(1, E) as e:
                    body(e)
                for i in range(E, ITEMS):
                    for kind, n in (("gate", FT), ("up", FT), ("down", TS)):
                        for j in range(n):
                            ffn(i, kind, j)
                pe.wait_ge(y_done, (c + 1) * (NS * TS))
                for g in range(G):
                    for s in range(TS):
                        last = pe.transpose(hT[g][:, s * P:(s + 1) * P], yacc[:, s, g * P:(g + 1) * P], eye_sb[:])
                    last.then_inc(yT_done, 1)
                pe.wait_ge(z_done, c * G + G)
                pe.wait_ge(comb_done, (c + 1) * (ITEMS * TS) + HEAD)
                for s in range(TS):
                    for k in range(G):
                        last = pe.matmul(pre_bank[s][:], xnT[:, k, s * P:(s + 1) * P], ow_sb[:, k, :],
                                         start=(k == 0), stop=(k == G - 1))
                    last.then_inc(s_done, 1)


def kernel(**inputs):
    import numpy as np
    import concourse.bacc as bacc
    from concourse.bass_utils import run_bass_kernel_spmd

    v = {k.removeprefix("L0_"): np.asarray(a) for k, a in inputs.items()}

    def tiles(a):
        return a.reshape(-1, P, *a.shape[1:]).swapaxes(0, 1)

    def both(r, s):
        return np.concatenate([v["ffn_" + r], v["ffn_" + s]], 0)

    def expert_rows(w):
        return w.reshape(ITEMS, -1, P, w.shape[2]).swapaxes(1, 2).reshape(ITEMS, P, -1)

    arrays = {
        "x": v["attn_x"].reshape(-1, DIM),
        "xpw": tiles(v["attn_x_proj_w"].T),
        "dtw": v["attn_dt_proj_w"].T,
        "wa": tiles(v["ffn_wa"]),
        "ow": tiles(v["attn_out_proj_w"].T),
        "cols": np.stack([v["attn_norm_w"], v["attn_norm_b"], v["attn_dt_proj_b"], v["attn_D_param"]])
        .reshape(4, G, P).transpose(2, 0, 1),
        "a_log": tiles(v["attn_A_log"]),
        "ew": np.concatenate([expert_rows(both(*p)) for p in (("rg", "sg"), ("rw1", "sw1"), ("rw2", "sw2"))], 2),
        "eb": np.stack([both("rgb", "sgb"), both("rb1", "sb1")]).reshape(2, ITEMS, FT, P).transpose(3, 0, 1, 2),
        "eb2": both("rb2", "sb2"),
        "eye": np.eye(P, dtype=np.float32),
        "iota": np.tile(np.arange(E, dtype=np.float32), (P, 1)),
    }
    arrays = {"in_" + k: np.ascontiguousarray(a) for k, a in arrays.items()}
    nc = bacc.Bacc("TRN2", target_bir_lowering=False, num_devices=1)
    args = [nc.dram_tensor(k, a.shape, mybir.dt.from_np(a.dtype), kind="ExternalInput").ap() for k, a in arrays.items()]
    args.append(nc.dram_tensor("out", [BATCH * SEQ, DIM], F32, kind="ExternalOutput").ap())
    build(nc, *args)
    r = run_bass_kernel_spmd(nc, [arrays], core_ids=[0])
    return r.results[0]["out"].reshape(BATCH, SEQ, DIM)
```

```python
from contextlib import ExitStack

import concourse.bass as bass
from concourse import mybir

F32 = mybir.dt.float32
U32 = mybir.dt.uint32
ALU = mybir.AluOpType
ACT = mybir.ActivationFunctionType
AX = mybir.AxisListType.X

P = 128
DIM = 512
G = DIM // P
T = 512
TS = T // P
BATCH, SEQ = 2, 2048
CPB = SEQ // T
CHUNKS = BATCH * CPB
TILES = CHUNKS * TS
NS = 64
RANK = 128
E, SH, F, TOPK = 16, 2, 256, 2
ITEMS = E + SH
FT = F // P
NPI = 4
ITERS = NS // NPI
BPC = 10
BLOCKS = BPC * CHUNKS
assert BLOCKS >= TOPK * TILES + E - 1 and BPC + SH <= ITERS
USES = BPC + SH
EPS = 1e-5
UNITS = NS * G
HEAD = 4
FFN = 2 * FT + TS

SHARED = {0: ("gate", 0, 0), 1: ("gate", 0, 1), 2: ("gate", 1, 0), 3: ("gate", 1, 1),
          6: ("up", 0, 0), 7: ("up", 0, 1), 8: ("up", 1, 0), 9: ("up", 1, 1),
          12: ("down", 0, 0), 13: ("down", 1, 0), 14: ("down", 2, 0), 15: ("down", 3, 0)}
ROUTED = {0: "tokens", 3: "gate_up", 10: "hidden", 12: "down"}
DVE_LINKS = 8


def build(nc, x, xpw, dtw, wa, ow, cols, a_log, ew, eb, ebr, eb2, eye, tri, iota, mask, bidx, be0, tokid, out):
    x_v = x.rearrange("(c s p) d -> c p s d", s=TS, p=P)
    out_v = out.rearrange("(c s p) d -> c p s d", s=TS, p=P)

    def dram(name, shape, dt=F32):
        return nc.dram_tensor(name, shape, dt, kind="Internal").ap()

    xn_dram = dram("xn_scratch", [BATCH * SEQ, DIM])
    s_dram = dram("s_scratch", [BATCH * SEQ, DIM])
    f_dram = dram("f_scratch", [BATCH * SEQ, DIM])
    y_dram = dram("y_scratch", [BLOCKS * P, DIM])
    tok_dram = dram("tok_scratch", [P * (BLOCKS + 1), 1], U32)
    bt_dram = dram("bt_scratch", [CHUNKS, NS, T])
    by_chunk = "(c s p) d -> c p s d"
    xn_v, s_v, f_v = (a.rearrange(by_chunk, s=TS, p=P) for a in (xn_dram, s_dram, f_dram))

    with ExitStack() as ctx:
        def sb(name, shape, dt=F32):
            return ctx.enter_context(nc.sbuf_tensor(name, shape, dt))

        def sem(name):
            return ctx.enter_context(nc.semaphore(name))

        xpw_sb = sb("xpw_sb", [P, G, RANK + 2 * NS])
        dtw_sb = sb("dtw_sb", [P, DIM])
        wa_sb = sb("wa_sb", [P, G, E])
        ow_sb = sb("ow_sb", [P, G, DIM])
        cols_sb = sb("cols_sb", [P, 4, G])
        nw, nb, dtb, dpar = (cols_sb[:, i, :] for i in range(4))
        A = sb("A", [P, G, NS])
        eb_sb = sb("eb_sb", [P, 2, SH, FT])
        eb2_sb = sb("eb2_sb", [ITEMS, DIM])
        eye_sb = sb("eye_sb", [P, P])
        tri_sb = sb("tri_sb", [P, P])
        ones_sb = sb("ones_sb", [P, P])
        iota_sb = sb("iota_sb", [P, E])
        mask_sb = sb("mask_sb", [P, E, TILES])
        bidx_sb = sb("bidx_sb", [1, BLOCKS, E])
        be0_sb = sb("be0_sb", [1, CHUNKS * (BPC + 1) + 1])
        tokid_sb = sb("tokid_sb", [P, TILES], U32)
        consts = ((xpw_sb, xpw), (dtw_sb, dtw), (wa_sb, wa), (ow_sb, ow), (cols_sb, cols), (A, a_log), (eb_sb, eb),
                  (eb2_sb, eb2), (eye_sb, eye), (tri_sb, tri), (iota_sb, iota), (mask_sb, mask), (bidx_sb, bidx),
                  (be0_sb, be0), (tokid_sb, tokid))
        nhalf = sb("nhalf", [P, TS])
        wgu = sb("wgu", [P, G, 2, F])
        wd = sb("wd", [P, FT, DIM])
        brow = sb("brow", [1, 2 * F])
        xn0 = sb("xn0", [P, TS, DIM])
        xh1 = sb("xh1", [P, TS, DIM])
        x0T = sb("x0T", [P, G, T])
        xnT = sb("xnT", [P, G, T])
        stats = sb("stats", [P, 2, TS, 6])
        mv = sb("mv", [P, 2, TS, 2])
        veps = sb("veps", [P, 2, TS])
        rstd = sb("rstd", [P, 2, TS])
        drT = sb("drT", [P, T])
        bT = sb("bT", [NS, T])
        cc = sb("cc", [P, TS, NS])
        sp = sb("sp", [P, G, T])
        spl = sb("spl", [P, G, T])
        facc = sb("facc", [P, TS, DIM])
        yacc = sb("yacc", [P, TS, DIM])
        state = sb("state", [P, G, NS])
        h = sb("h", [P, 2, G, T])
        dbx = sb("dbx", [P, G, T])
        bbc = sb("bbc", [P, NPI, T])
        hg = sb("hg", [P, FT, T])
        hid = sb("hid", [P, FT, T])
        aff = sb("aff", [P, TILES, E])
        top = sb("top", [P, TOPK, TILES])
        pick = sb("pick", [P, TOPK, TILES])
        rsum = sb("rsum", [P, TILES])
        W = sb("W", [P, TILES, ITEMS])
        Wc = sb("Wc", [P, TS, ITEMS])
        WT = sb("WT", [ITEMS, T])
        per_e = sb("per_e", [P, 4, E])
        per_e_u = sb("per_e_u", [P, E], U32)
        slot_f = sb("slot_f", [P, TOPK, TILES])
        slot_u = sb("slot_u", [P, TOPK, TILES], U32)
        part_u = sb("part_u", [P, 2, TOPK, TILES], U32)
        part_f = sb("part_f", [P, 2, TOPK, TILES])
        tpos_u = sb("tpos_u", [P, TOPK, TILES], U32)
        be_u = sb("be_u", [1, CHUNKS * (BPC + 1) + 1], U32)
        scat_i = sb("scat_i", [P, TOPK, 8], U32)
        scat_t = sb("scat_t", [P, 8], U32)
        tok_sb = sb("tok_sb", [P, BLOCKS + 1], U32)
        idx = sb("idx", [P, 1], U32)
        xg = sb("xg", [P, DIM])
        xgT = sb("xgT", [P, G, P])
        hgr = sb("hgr", [P, F])
        hidr = sb("hidr", [P, F])
        hidrT = sb("hidrT", [P, FT, P])
        yo = sb("yo", [P, DIM])
        x_b = (yacc, sp)
        n_b = (facc, spl)
        t_b = (x0T, xnT)
        x4, s4, f4, r4 = (xn0, xh1), (x0T, xnT), (facc, yacc), ((sp, spl), (h[:, 0], h[:, 1]))
        idx4 = sb("idx4", [P, 2, TOPK, TS], U32)
        eq, cand, aff2, pos = (dbx[:, i, :].rearrange("p (t e) -> p t e", e=E) for i in range(4))
        O = [bbc[:, j, :].rearrange("p (t e) -> p t e", e=E) for j in range(TOPK)]
        Osum, Wtmp = (bbc[:, j, :].rearrange("p (t e) -> p t e", e=E) for j in (2, 3))
        cnt, cum, excl = (a.rearrange("p (e t) -> p e t", e=E) for a in (hg[:, 0, :], hg[:, 1, :], hid[:, 0, :]))
        bcmp = h[0:1, 0].rearrange("p a b -> p (a b)")[:, 0:BLOCKS * E].rearrange("p (b e) -> p b e", e=E)

        hT = [ctx.enter_context(nc.psum_tensor(f"hT{i}", [P, 512], F32)) for i in range(TS)]
        dA = [ctx.enter_context(nc.psum_tensor(f"dA{i}", [P, 512], F32)) for i in range(2)]
        FP = [ctx.enter_context(nc.psum_tensor(f"FP{i}", [P, 512], F32)) for i in range(2)]
        pre_bank = [dA[0], dA[1], FP[0], FP[1]]

        const_in = sem("const_in")
        dve_const = sem("dve_const")
        passed = sem("passed")
        a_exp = sem("a_exp")
        x_in = [sem(f"x_in{i}") for i in range(2)]
        xn_out = [sem(f"xn_out{i}") for i in range(2)]
        p1_bn = sem("p1_bn")
        p1_stats = sem("p1_stats")
        p1_add = sem("p1_add")
        p1_rstd = sem("p1_rstd")
        p1_norm = sem("p1_norm")
        p1_tr = sem("p1_tr")
        p1_cp = sem("p1_cp")
        p1_log = sem("p1_log")
        p1_exp = sem("p1_exp")
        r_link = sem("r_link")
        picked = sem("picked")
        rank_done = sem("rank_done")
        tok0_out = sem("tok0_out")
        slot_done = sem("slot_done")
        scat_copy = sem("scat_copy")
        scat_out = sem("scat_out")
        tok_in = sem("tok_in")
        be_done = sem("be_done")
        n_in = sem("n_in")
        bt_out = sem("bt_out")
        dve_link = sem("dve_link")
        stats_done = sem("stats_done")
        rstd_add = sem("rstd_add")
        rstd_done = sem("rstd_done")
        norm_done = sem("norm_done")
        tr_done = sem("tr_done")
        trc_done = sem("trc_done")
        proj_done = sem("proj_done")
        projc_done = sem("projc_done")
        cc_done = sem("cc_done")
        pre_done = sem("pre_done")
        abs_done = sem("abs_done")
        relu_done = sem("relu_done")
        spe_done = sem("spe_done")
        ln_done = sem("ln_done")
        delta_done = sem("delta_done")
        u_done = sem("u_done")
        wc_done = sem("wc_done")
        wt_done = sem("wt_done")
        wtc_done = sem("wtc_done")
        bias_done = sem("bias_done")
        facc_done = sem("facc_done")
        b_in = [sem(f"b_in{i}") for i in range(NPI)]
        exp_done = sem("exp_done")
        dbx_done = sem("dbx_done")
        scan_done = sem("scan_done")
        hT_done = sem("hT_done")
        y_done = sem("y_done")
        state_done = sem("state_done")
        gu_in, wd_in = sem("gu_in"), sem("wd_in")
        xg_in = sem("xg_in")
        idx_done = sem("idx_done")
        blk_pe = sem("blk_pe")
        blk_act = sem("blk_act")
        blk_dve = sem("blk_dve")
        yo_out = sem("yo_out")
        ffn_done = sem("ffn_done")
        gelu_done = sem("gelu_done")
        hid_done = sem("hid_done")
        comb_done = sem("comb_done")
        yT_done = sem("yT_done")
        z_done = sem("z_done")
        s_done = sem("s_done")
        sc_done = sem("sc_done")
        sf_out = sem("sf_out")
        in4 = [sem(f"in4_{i}") for i in range(2)]
        idx4_done = sem("idx4_done")
        rows4 = [sem(f"rows4_{i}") for i in range(2)]
        f4_done = sem("f4_done")
        silu_done = sem("silu_done")
        g4_done = sem("g4_done")
        o4_done = sem("o4_done")
        out_dma = [sem(f"out_dma{i}") for i in range(2)]

        block = ctx.enter_context(nc.Block())

        def wait_alone(eng, sem, value):
            eng.wait_ge(sem, value)
            eng.sem_inc(passed, 1)

        @block.sync
        def _(sp):
            for dst, src in consts:
                sp.dma_start(dst[:], src).then_inc(const_in, 16)
            for p in range(2):
                sp.sem_inc(xn_out[p], HEAD)
                sp.sem_inc(out_dma[p], HEAD)
                sp.dma_start(x_b[p][:], x_v[p]).then_inc(x_in[p], 16)

            def phase1(c, p, more=True):
                sp.wait_ge(p1_norm, c + 1)
                sp.dma_start(xn_v[c], n_b[p][:]).then_inc(xn_out[p], 16)
                if more:
                    sp.dma_start(x_b[p][:], x_v[c + 2]).then_inc(x_in[p], 16)

            with sp.Fori(0, CHUNKS // 2 - 1) as cp:
                for p in range(2):
                    phase1(cp * 2 + p, p)
            for p in range(2):
                phase1(CHUNKS - 2 + p, p, False)
            sp.wait_ge(dve_const, 5)
            sp.dma_start(tok_dram.rearrange("(p b) o -> p (b o)", p=P), tok_sb[:]).then_inc(tok0_out, 16)
            for p in range(2):
                sp.wait_ge(xn_out[p], CHUNKS // 2 * 16 + HEAD)

            def expert(use):
                return sp.value_load(be_u[0:1, bass.ds(use, 1)], min_val=0, max_val=ITEMS - 1)

            def load_gu(i):
                sp.dma_start(wgu[:], ew[bass.ds(i, 1), :, 0:2 * G * F].rearrange("o p (k g f) -> (o p) k g f", k=G, g=2))\
                    .then_inc(gu_in, 16)
                sp.dma_start(brow[:], ebr[bass.ds(i, 1), :]).then_inc(gu_in, 16)

            def load_wd(i):
                sp.dma_start(wd[:], ew[bass.ds(i, 1), :, 2 * G * F:].rearrange("o p (k d) -> (o p) k d", k=FT))\
                    .then_inc(wd_in, 16)

            def load_b(c, n, j):
                sp.dma_start(bbc[:, j, :], bt_dram[c, n, :].partition_broadcast(P)).then_inc(b_in[j], 16)

            sp.wait_ge(be_done, 1)
            load_gu(expert(0))
            sp.wait_ge(scat_out, TOPK * TILES * 16)
            sp.dma_start(tok_sb[:], tok_dram.rearrange("(p b) o -> p (b o)", p=P)).then_inc(tok_in, 16)
            sp.wait_ge(slot_done, 1)
            with sp.Fori(0, CHUNKS) as c:
                sp.dma_start(xn0[:], xn_v[c]).then_inc(n_in, 16)
                sp.wait_ge(projc_done, c * 2 + 2)
                sp.dma_start(bt_dram[c], bT[:]).then_inc(bt_out, 16)
                sp.wait_ge(bt_out, c * 16 + 16)
                for j in range(NPI):
                    load_b(c, j, j)

                def body(i, kind=None, last=False):
                    for k in range(NPI):
                        if not last:
                            sp.wait_ge(dbx_done, c * UNITS + i * (NPI * G) + (k + 1) * G)
                            load_b(c, i * NPI + NPI + k, k)
                        if kind and k == 1:
                            if kind == "routed":
                                sp.wait_ge(ffn_done, c * (SH * FFN) + 1)
                                sp.wait_ge(blk_pe, (c * BPC + i) * 4 + 1)
                            elif i == ITERS - SH:
                                sp.wait_ge(blk_pe, (c + 1) * (BPC * 4) + 1)
                            else:
                                sp.wait_ge(ffn_done, (c * SH + i - ITERS + SH) * FFN + 1)
                            load_wd(expert(c * (BPC + 1) + i) if kind == "routed" else E + i - ITERS + SH)
                        if kind and k == 2:
                            if kind == "routed":
                                sp.wait_ge(blk_pe, (c * BPC + i) * 4 + 3)
                            else:
                                sp.wait_ge(ffn_done, (c * SH + i - ITERS + SH) * FFN + 2 * FT + 1)
                            if kind == "routed":
                                load_gu(expert(c * (BPC + 1) + i + 1))
                            elif not last:
                                load_gu(E + i - ITERS + SH + 1)
                            else:
                                load_gu(expert((c + 1) * (BPC + 1)))

                with sp.Fori(0, BPC) as i:
                    body(i, "routed")
                with sp.Fori(BPC, ITERS - SH) as i:
                    body(i)
                for i in range(ITERS - SH, ITERS):
                    body(i, "shared", i == ITERS - 1)
                sp.wait_ge(comb_done, (c + 1) * (SH * TS) + HEAD)
                sp.dma_start(f_v[c], facc[:]).then_inc(sf_out, 16)
                sp.wait_ge(sc_done, c * TS + TS)
                sp.dma_start(s_v[c], xh1[:]).then_inc(sf_out, 16)
                wait_alone(sp, sf_out, c * 32 + 32)

            def load4(c, p):
                sp.dma_start(x4[p][:], x_v[c]).then_inc(in4[p], 16)
                sp.dma_start(s4[p][:], s_v[c]).then_inc(in4[p], 16)
                sp.dma_start(f4[p][:], f_v[c]).then_inc(in4[p], 16)

            sp.wait_ge(z_done, CHUNKS * G)
            sp.wait_ge(s_done, CHUNKS * TS)
            for p in range(2):
                load4(p, p)

            def phase4(c, cp, p, more=True):
                sp.wait_ge(o4_done, c + 3)
                sp.dma_start(out_v[c], x4[p][:]).then_inc(out_dma[p], 16)
                if more:
                    sp.wait_ge(out_dma[p], cp * 16 + 16 + HEAD)
                    load4(c + 2, p)

            with sp.Fori(0, CHUNKS // 2 - 1) as cp:
                for p in range(2):
                    phase4(cp * 2 + p, cp, p)
            for p in range(2):
                phase4(CHUNKS - 2 + p, CHUNKS // 2 - 1, p, False)
            for p in range(2):
                sp.wait_ge(out_dma[p], CHUNKS // 2 * 16 + HEAD)
            sp.wait_ge(yo_out, BLOCKS * 16 + HEAD)
            sp.wait_ge(sf_out, CHUNKS * 32)
            sp.wait_ge(xg_in, BLOCKS * 16 + 16)
            sp.wait_ge(gu_in, CHUNKS * USES * 32 + 32)

        @block.gpsimd
        def _(pool):
            pool.wait_ge(dve_const, 1)

            def rsqrt(p, stats_sem, add_sem, done, n):
                wait_alone(pool, stats_sem, n)
                pool.tensor_scalar(veps[:, p, :], mv[:, p, :, 1], EPS, None, ALU.add).then_inc(add_sem, 1)
                pool.wait_ge(add_sem, n)
                pool.tensor_tensor(rstd[:, p, :], veps[:, p, :], nhalf[:], ALU.pow).then_inc(done, 1)

            with pool.Fori(0, CHUNKS // 2) as cp:
                for p in range(2):
                    rsqrt(p, p1_stats, p1_add, p1_rstd, cp * 2 + (p + 1))

            pool.wait_ge(slot_done, 1)
            pool.wait_ge(tok0_out, 16)
            with pool.Fori(0, TILES // 8) as i:
                for j in range(TOPK):
                    pool.tensor_copy(scat_i[:, j, :], tpos_u[:, j, bass.ds(i * 8, 8)])
                pool.tensor_copy(scat_t[:], tokid_sb[:, bass.ds(i * 8, 8)]).then_inc(scat_copy, 1)
                wait_alone(pool, scat_copy, i + 1)
                for q in range(8):
                    for j in range(TOPK):
                        pool.indirect_dma_start(tok_dram, bass.IndirectOffsetOnAxis(scat_i[:, j, q:q + 1], 0),
                                                scat_t[:, q:q + 1], None).then_inc(scat_out, 16)
                wait_alone(pool, scat_out, (i + 1) * (TOPK * 8 * 16))

            def gather(v):
                pool.tensor_copy(idx[:], tok_sb[:, bass.ds(v, 1)]).then_inc(idx_done, 1)
                wait_alone(pool, idx_done, v + 1)
                pool.indirect_dma_start(xg[:], None, xn_dram, bass.IndirectOffsetOnAxis(idx[:, 0:1], 0))\
                    .then_inc(xg_in, 16)

            pool.wait_ge(tok_in, 16)
            for p in range(2):
                pool.wait_ge(xn_out[p], CHUNKS // 2 * 16 + HEAD)
            gather(0)
            with pool.Fori(0, CHUNKS) as c:
                rsqrt(0, stats_done, rstd_add, rstd_done, c + 1)
                wait_alone(pool, u_done, c + 1)

                def body(i, routed=False):
                    for k in range(NPI):
                        pool.wait_ge(b_in[k], c * (ITERS * 16) + i * 16 + 16)
                        for g in range(G):
                            pool.wait_ge(scan_done, c * UNITS + i * (NPI * G) + (k * G + g - G + 1) + HEAD)
                            pool.tensor_tensor(dbx[:, g, :], spl[:, g, :], bbc[:, k, :], ALU.mult)\
                                .then_inc(dbx_done, 1)
                        if routed and k == 2:
                            wait_alone(pool, blk_pe, (c * BPC + i) * 4 + 2)
                            gather(c * BPC + i + 1)

                with pool.Fori(0, BPC) as i:
                    body(i, True)
                with pool.Fori(BPC, ITERS) as i:
                    body(i)

            pool.wait_ge(yo_out, BLOCKS * 16 + HEAD)
            pool.wait_ge(z_done, CHUNKS * G)
            with pool.Fori(0, CHUNKS // 2) as cp:
                for p in range(2):
                    c = cp * 2 + p
                    wait_alone(pool, o4_done, c + 1)
                    for j in range(TOPK):
                        last = pool.tensor_copy(idx4[:, p, j, :], slot_u[:, j, bass.ds(c * TS, TS)])
                    last.then_inc(idx4_done, 1)
                    wait_alone(pool, idx4_done, c + 1)
                    for s in range(TS):
                        for j in range(TOPK):
                            pool.indirect_dma_start(r4[p][j][:, s, :], None, y_dram,
                                                    bass.IndirectOffsetOnAxis(idx4[:, p, j, s:s + 1], 0))\
                                .then_inc(rows4[p], 16)

        @block.scalar
        def _(act):
            act.wait_ge(const_in, 16 * len(consts))
            act.activation(A[:], A[:], ACT.Exp).then_inc(a_exp, 1)
            act.sem_inc(p1_exp, 2)
            act.sem_inc(blk_act, 1)
            act.sem_inc(yo_out, HEAD)
            with act.Fori(0, CHUNKS // 2) as cp:
                for p in range(2):
                    c = cp * 2 + p
                    banks = (hT, pre_bank)[p]
                    for g in range(G):
                        act.wait_ge(p1_tr, c * G + (g + 1 + 2 * G))
                        act.activation(t_b[p][:, g, :], banks[g][:], ACT.Copy).then_inc(p1_cp, 1)
                    act.wait_ge(p1_log, c + 1)
                    act.activation(aff[:, bass.ds(c * TS, TS), :],
                                   banks[0][:, 0:TS * E].rearrange("p (s e) -> p s e", s=TS), ACT.Exp,
                                   scale=-1.0).then_inc(p1_exp, 1)
            act.wait_ge(dve_const, 3)
            act.wait_ge(slot_done, 1)
            with act.Fori(0, CHUNKS) as c:
                act.activation(Wc[:], W[:, bass.ds(c * TS, TS), :], ACT.Copy).then_inc(wc_done, 1)
                for g in range(G):
                    act.wait_ge(tr_done, c * (2 * G) + g + 1)
                    act.activation(x0T[:, g, :], hT[g][:], ACT.Copy).then_inc(trc_done, 1)
                for g in range(G):
                    act.wait_ge(tr_done, c * (2 * G) + G + g + 1)
                    act.activation(xnT[:, g, :], pre_bank[g][:], ACT.Identity, scale=nw[:, g:g + 1],
                                   bias=nb[:, g:g + 1]).then_inc(trc_done, 1)
                act.wait_ge(proj_done, c * 3 + 1)
                act.activation(drT[:], hT[0][:], ACT.Copy).then_inc(projc_done, 1)
                act.wait_ge(proj_done, c * 3 + 2)
                act.activation(bT[:], hT[1][0:NS, :], ACT.Copy).then_inc(projc_done, 1)
                for g in range(G):
                    act.wait_ge(pre_done, c * G + g + 1)
                    act.activation(spl[:, g, :], pre_bank[g][:], ACT.Abs, bias=dtb[:, g:g + 1]).then_inc(abs_done, 1)
                act.wait_ge(abs_done, c * G + G)
                act.activation(spl[:], spl[:], ACT.Exp, scale=-1.0).then_inc(spe_done, 1)
                act.wait_ge(spe_done, c + 1)
                act.activation(spl[:], spl[:], ACT.Ln, bias=1.0).then_inc(ln_done, 1)
                act.wait_ge(wt_done, c + 1)
                act.activation(WT[:], dA[0][0:ITEMS, :], ACT.Copy).then_inc(wtc_done, 1)
                act.wait_ge(delta_done, c + 1)
                act.wait_ge(wtc_done, c + 1)

                def gelu(s, f):
                    act.wait_ge(ffn_done, (c * SH + s) * FFN + f + 2)
                    act.activation(hg[:, f, :], FP[f][:], ACT.Gelu, bias=eb_sb[:, 0, s, f:f + 1])\
                        .then_inc(gelu_done, 1)

                def step(n, k, block=None, shared=None):
                    for g in range(G):
                        act.wait_ge(scan_done, c * UNITS + n * G + (g - 1) + HEAD)
                        act.activation(dA[g % 2][:], sp[:, g, :], ACT.Exp, scale=A[:, g, bass.ds(n, 1)])\
                            .then_inc(exp_done, 1)
                        if block is not None and (k, g) == (1, 2):
                            act.wait_ge(blk_pe, block * 4 + 2)
                            act.activation(xgT[:], FP[0][:].rearrange("p (k t) -> p k t", k=G), ACT.Copy)\
                                .then_inc(blk_act, 1)
                        if block is not None and (k, g) == (3, 0):
                            act.wait_ge(blk_pe, block * 4 + 3)
                            act.activation(hgr[:], FP[1][:, 0:F], ACT.Gelu).then_inc(blk_act, 1)
                        if block is not None and (k, g) == (0, 2):
                            act.wait_ge(yo_out, block * 16 + HEAD)
                            act.wait_ge(blk_pe, block * 4 + 5)
                            act.activation(yo[:], FP[1][:], ACT.Copy).then_inc(blk_act, 1)
                        if block is not None and (k, g) == (0, 3):
                            act.wait_ge(blk_act, block * 3 + 4)
                            act.dma_start(y_dram[bass.ds(block * P, P), :], yo[:]).then_inc(yo_out, 16)
                        if shared is not None and (k, g) == (2, 1):
                            for f in range(FT):
                                gelu(shared, f)

                step(0, 0)
                with act.Fori(0, BPC) as i:
                    for k in range(1, NPI + 1):
                        step(i * NPI + k, k % NPI, block=c * BPC + i)
                with act.Fori(BPC, ITERS - SH) as i:
                    for k in range(1, NPI + 1):
                        step(i * NPI + k, k % NPI)
                for i in range(ITERS - SH, ITERS):
                    for k in range(1, NPI + (i < ITERS - 1)):
                        step(i * NPI + k, k % NPI, shared=i - ITERS + SH)
                for s in range(TS):
                    act.wait_ge(s_done, c * TS + s + 1)
                    act.activation(xh1[:, s, :], pre_bank[s][:], ACT.Copy).then_inc(sc_done, 1)
            with act.Fori(0, CHUNKS // 2) as cp:
                for p in range(2):
                    act.wait_ge(f4_done, (cp * 2 + p) * TOPK + TOPK)
                    act.activation(f4[p][:], f4[p][:], ACT.Silu).then_inc(silu_done, 1)

        @block.vector
        def _(dve):
            dve.memset(nhalf[:], -0.5).then_inc(dve_const, 1)
            dve.memset(W[:], 1.0)
            dve.memset(ones_sb[:], 1.0)
            dve.memset(per_e[:, 2, :], 1.0).then_inc(dve_const, 1)
            for done, n in ((scan_done, HEAD), (comb_done, HEAD), (y_done, HEAD), (blk_dve, 1), (o4_done, 2)):
                dve.sem_inc(done, n)
            dve.wait_ge(a_exp, 1)
            dve.tensor_scalar(A[:], A[:], -1.0, None, ALU.mult).then_inc(dve_const, 1)
            dve.memset(tok_sb[:], 0).then_inc(dve_const, 2)
            dve.wait_ge(dve_const, 5)

            with dve.Fori(0, CHUNKS // 2) as cp:
                for p in range(2):
                    c = cp * 2 + p
                    wait_alone(dve, x_in[p], cp * 16 + 16)
                    for s in range(TS):
                        last = dve.bn_stats(stats[:, p, s, :], x_b[p][:, s, :])
                    last.then_inc(p1_bn, 1)
                    wait_alone(dve, p1_bn, c + 1)
                    for s in range(TS):
                        last = dve.bn_aggr(mv[:, p, s, :], stats[:, p, s, :])
                    last.then_inc(p1_stats, 1)
                    dve.wait_ge(p1_rstd, c + 1)
                    dve.wait_ge(xn_out[p], cp * 16 + HEAD)
                    dve.wait_ge(p1_tr, c * G + G)
                    for s in range(TS):
                        last = dve.tensor_scalar(n_b[p][:, s, :], x_b[p][:, s, :], mv[:, p, s, 0:1], rstd[:, p, s:s + 1],
                                                 ALU.subtract, ALU.mult)
                    last.then_inc(p1_norm, 1)

            steps = [0]

            def link(ins):
                steps[0] += 1
                ins.then_inc(r_link, 1)
                dve.wait_ge(r_link, steps[0])

            def over_e(a):
                return a.unsqueeze(2).to_broadcast([P, TILES, E])

            def over_t(a):
                return a.unsqueeze(1).to_broadcast([P, TILES, E])

            dve.wait_ge(p1_exp, CHUNKS + 2)
            dve.wait_ge(p1_tr, CHUNKS * G + 2 * G)
            link(dve.tensor_scalar(aff[:], aff[:], 1.0, None, ALU.add))
            link(dve.reciprocal(aff[:], aff[:]))
            src = aff[:]
            for j in range(TOPK):
                link(dve.tensor_reduce(top[:, j, :], src, AX, ALU.max))
                link(dve.tensor_tensor(eq, src, over_e(top[:, j, :]), ALU.is_equal))
                link(dve.scalar_tensor_tensor(cand, eq, float(-E), over_t(iota_sb[:]), ALU.mult, ALU.add))
                link(dve.tensor_reduce(pick[:, j, :], cand, AX, ALU.min))
                link(dve.tensor_tensor(O[j], cand, over_e(pick[:, j, :]), ALU.is_equal))
                if j == 0:
                    link(dve.scalar_tensor_tensor(aff2, O[0], -4.0, aff[:], ALU.mult, ALU.add))
                    src = aff2
            link(dve.tensor_tensor(Osum, O[0], O[1], ALU.add))
            dve.sem_inc(picked, 1)
            link(dve.tensor_tensor(rsum[:], top[:, 0, :], top[:, 1, :], ALU.add))
            link(dve.reciprocal(rsum[:], rsum[:]))
            for j in range(TOPK):
                link(dve.tensor_tensor(top[:, j, :], top[:, j, :], rsum[:], ALU.mult))
            link(dve.tensor_tensor(eq, O[0], over_e(top[:, 0, :]), ALU.mult))
            link(dve.tensor_tensor(Wtmp, O[1], over_e(top[:, 1, :]), ALU.mult))
            link(dve.tensor_tensor(W[:, :, 0:E], eq, Wtmp, ALU.add))
            dve.wait_ge(rank_done, 2)
            link(dve.tensor_copy(cnt, hT[1][:].rearrange("p (t e) -> p e t", e=E)))
            flat = "p e t -> p (e t)"
            link(dve.tensor_tensor_scan(cum.rearrange(flat), mask_sb[:].rearrange(flat), cnt.rearrange(flat), 0.0,
                                        ALU.mult, ALU.add))
            link(dve.tensor_tensor(excl, cum, cnt, ALU.subtract))
            link(dve.tensor_scalar(per_e_u[:], cum[:, :, TILES - 1], float(P - 1), None, ALU.add))
            link(dve.tensor_scalar(per_e_u[:], per_e_u[:], 7, None, ALU.logical_shift_right))
            link(dve.tensor_copy(per_e[:, 0, :], per_e_u[:]))
            link(dve.tensor_tensor_scan(per_e[:, 1, :], per_e[:, 2, :], per_e[:, 0, :], 0.0, ALU.mult, ALU.add))
            link(dve.tensor_tensor(per_e[:, 3, :], per_e[:, 1, :], per_e[:, 0, :], ALU.subtract))
            link(dve.tensor_scalar(per_e[:, 3, :], per_e[:, 3, :], float(P), None, ALU.mult))
            link(dve.tensor_tensor(bcmp, bidx_sb[:], per_e[0:1, 1, :].unsqueeze(1).to_broadcast([1, BLOCKS, E]),
                                   ALU.is_ge))
            routed = be0_sb[:, 0:CHUNKS * (BPC + 1)].rearrange("o (c b) -> o c b", c=CHUNKS)[:, :, 0:BPC]
            link(dve.tensor_reduce(routed, bcmp.rearrange("o (c b) e -> o c b e", c=CHUNKS), AX, ALU.add))
            link(dve.tensor_scalar(routed, routed, float(E - 1), None, ALU.min))
            link(dve.tensor_copy(be_u[:], be0_sb[:]))
            dve.sem_inc(be_done, 1)
            link(dve.tensor_tensor(pos, hT[0][:].rearrange("p (t e) -> p t e", e=E), excl.rearrange("p e t -> p t e"),
                                   ALU.add))
            link(dve.tensor_tensor(pos, pos, over_t(per_e[:, 3, :]), ALU.add))
            for j in range(TOPK):
                link(dve.tensor_tensor(eq, O[j], pos, ALU.mult))
                link(dve.tensor_reduce(slot_f[:, j, :], eq, AX, ALU.add))
            link(dve.tensor_copy(slot_u[:], slot_f[:]))
            link(dve.tensor_scalar(part_u[:, 0], slot_u[:], P - 1, None, ALU.bitwise_and))
            link(dve.tensor_scalar(part_u[:, 1], slot_u[:], 7, None, ALU.logical_shift_right))
            link(dve.tensor_copy(part_f[:], part_u[:]))
            link(dve.scalar_tensor_tensor(slot_f[:], part_f[:, 0], float(BLOCKS + 1), part_f[:, 1], ALU.mult, ALU.add))
            link(dve.tensor_copy(tpos_u[:], slot_f[:]))
            dve.sem_inc(slot_done, 1)

            with dve.Fori(0, BATCH) as b:
                dve.memset(state[:], 0.0)
                with dve.Fori(0, CPB) as cb:
                    c = b * CPB + cb
                    links = [0]

                    def clink(ins):
                        links[0] += 1
                        ins.then_inc(dve_link, 1)
                        wait_alone(dve, dve_link, c * DVE_LINKS + links[0])

                    wait_alone(dve, n_in, c * 16 + 16)
                    for s in range(TS):
                        last = dve.bn_stats(stats[:, 0, s, :], xn0[:, s, :])
                    clink(last)
                    for s in range(TS):
                        last = dve.bn_aggr(mv[:, 0, s, :], stats[:, 0, s, :])
                    last.then_inc(stats_done, 1)
                    dve.wait_ge(rstd_done, c + 1)
                    for s in range(TS):
                        last = dve.tensor_scalar(xh1[:, s, :], xn0[:, s, :], mv[:, 0, s, 0:1], rstd[:, 0, s:s + 1],
                                                 ALU.subtract, ALU.mult)
                    last.then_inc(norm_done, 1)
                    dve.wait_ge(proj_done, c * 3 + 3)
                    dve.tensor_copy(cc[:], hT[2][:, 0:TS * NS].rearrange("p (s n) -> p s n", s=TS)).then_inc(cc_done, 1)
                    for g in range(G):
                        dve.wait_ge(abs_done, c * G + g + 1)
                        dve.tensor_scalar(sp[:, g, :], pre_bank[g][:], dtb[:, g:g + 1], 0.0, ALU.add, ALU.max)\
                            .then_inc(relu_done, 1)
                    dve.wait_ge(relu_done, c * G + G)
                    dve.wait_ge(ln_done, c + 1)
                    dve.tensor_tensor(sp[:], sp[:], spl[:], ALU.add).then_inc(delta_done, 1)
                    dve.wait_ge(delta_done, c + 1)
                    dve.tensor_tensor(spl[:], sp[:], xnT[:], ALU.mult).then_inc(u_done, 1)
                    clink(dve.memset(yacc[:], 0.0))
                    for s in range(TS):
                        dve.wait_ge(bias_done, c * TS + s + 1)
                        dve.tensor_tensor(facc[:, s, :], hT[s][:], xn0[:, s, :], ALU.add).then_inc(facc_done, 1)
                    dve.wait_ge(facc_done, c * TS + TS)

                    def scan(n, k, g):
                        unit = n * G + g
                        dve.wait_ge(exp_done, c * UNITS + unit + 1)
                        dve.wait_ge(dbx_done, c * UNITS + unit + 1)
                        dve.tensor_tensor_scan(h[:, k % 2, g, :], dA[g % 2][:], dbx[:, g, :],
                                               state[:, g, bass.ds(n, 1)], ALU.mult, ALU.add).then_inc(scan_done, 1)

                    def y_add(n, s):
                        dve.wait_ge(hT_done, c * (NS * TS) + n * TS + s + 1)
                        dve.wait_ge(y_done, c * (NS * TS) + n * TS + s + 1 - TS + HEAD)
                        dve.scalar_tensor_tensor(yacc[:, s, :], hT[s][:], cc[:, s, bass.ds(n, 1)], yacc[:, s, :],
                                                 ALU.mult, ALU.add).then_inc(y_done, 1)

                    def keep_state(n, k):
                        wait_alone(dve, scan_done, c * UNITS + n * G + G + HEAD)
                        dve.tensor_copy(state[:, :, bass.ds(n, 1)], h[:, k % 2, :, T - 1:T]).then_inc(state_done, 1)

                    def hidden(i, f):
                        dve.wait_ge(ffn_done, (c * SH + i) * FFN + FT + f + 2)
                        dve.wait_ge(gelu_done, (c * SH + i) * FT + f + 1)
                        dve.scalar_tensor_tensor(hid[:, f, :], FP[f][:], eb_sb[:, 1, i, f:f + 1], hg[:, f, :],
                                                 ALU.add, ALU.mult).then_inc(hid_done, 1)

                    def combine(i, s):
                        dve.wait_ge(ffn_done, (c * SH + i) * FFN + 2 * FT + s + 2)
                        dve.wait_ge(comb_done, (c * SH + i) * TS + s + 1 - TS + HEAD)
                        dve.tensor_tensor(facc[:, s, :], FP[s % 2][:], facc[:, s, :], ALU.add).then_inc(comb_done, 1)

                    def step(n, k, block=None, shared=None, first=False):
                        scan(n, k, 0)
                        scan(n, k, 1)
                        if not first:
                            y_add(n - 1, 0)
                        scan(n, k, 2)
                        if not first:
                            y_add(n - 1, 1)
                        if shared is not None and k == 0:
                            combine(shared, 0)
                            combine(shared, 1)
                        if block is not None and k == 3:
                            dve.wait_ge(blk_act, block * 3 + 3)
                            dve.tensor_tensor(hidr[:], FP[1][:, F:2 * F], hgr[:], ALU.mult).then_inc(blk_dve, 1)
                        scan(n, k, 3)
                        if shared is not None and k == 3:
                            hidden(shared, 0)
                        if not first:
                            y_add(n - 1, 2)
                            y_add(n - 1, 3)
                        if shared is not None and k == 3:
                            hidden(shared, 1)
                        if block is not None and k == 3:
                            wait_alone(dve, blk_pe, block * 4 + 4)
                            dve.tensor_copy(hidrT[:], FP[0][:, 0:F].rearrange("p (f t) -> p f t", f=FT))\
                                .then_inc(blk_dve, 1)
                        if shared is not None and k == 0:
                            combine(shared, 2)
                            combine(shared, 3)
                        keep_state(n, k)

                    step(0, 0, first=True)
                    with dve.Fori(0, BPC) as i:
                        for k in range(1, NPI + 1):
                            step(i * NPI + k, k % NPI, block=c * BPC + i)
                    with dve.Fori(BPC, ITERS - SH) as i:
                        for k in range(1, NPI + 1):
                            step(i * NPI + k, k % NPI)
                    for i in range(ITERS - SH, ITERS):
                        for k in range(1, NPI + (i < ITERS - 1)):
                            step(i * NPI + k, k % NPI, shared=i - ITERS + SH)
                    for s in (0, 2):
                        y_add(NS - 1, s)
                        y_add(NS - 1, s + 1)
                        combine(SH - 1, s)
                        combine(SH - 1, s + 1)

                    for g in range(G):
                        dve.wait_ge(yT_done, c * G + g + 1)
                        dve.scalar_tensor_tensor(xnT[:, g, :], x0T[:, g, :], dpar[:, g:g + 1], hT[g][:],
                                                 ALU.mult, ALU.add).then_inc(z_done, 1)
                    dve.sem_inc(dve_link, DVE_LINKS - links[0])

            with dve.Fori(0, CHUNKS // 2) as cp:
                for p in range(2):
                    c = cp * 2 + p
                    dve.wait_ge(in4[p], cp * 48 + 48)
                    dve.wait_ge(rows4[p], (cp + 1) * (TOPK * TS * 16))
                    for j in range(TOPK):
                        for s in range(TS):
                            last = dve.scalar_tensor_tensor(f4[p][:, s, :], r4[p][j][:, s, :],
                                                            top[:, j, bass.ds(c * TS + s, 1)], f4[p][:, s, :],
                                                            ALU.mult, ALU.add)
                        last.then_inc(f4_done, 1)
                        dve.wait_ge(f4_done, c * TOPK + j + 1)
                    dve.wait_ge(silu_done, c + 1)
                    dve.tensor_tensor(s4[p][:], s4[p][:], f4[p][:], ALU.mult).then_inc(g4_done, 1)
                    dve.wait_ge(g4_done, c + 1)
                    dve.tensor_tensor(x4[p][:], x4[p][:], s4[p][:], ALU.add).then_inc(o4_done, 1)

        @block.tensor
        def _(pe):
            pe.wait_ge(const_in, 16 * len(consts))
            pe.wait_ge(dve_const, 2)
            pe.sem_inc(p1_tr, 2 * G)
            pe.sem_inc(blk_pe, 1)
            pe.sem_inc(ffn_done, 1)
            with pe.Fori(0, CHUNKS // 2) as cp:
                for p in range(2):
                    c = cp * 2 + p
                    banks = (hT, pre_bank)[p]
                    pe.wait_ge(p1_norm, c + 1)
                    pe.wait_ge(p1_exp, c + 1)
                    for g in range(G):
                        for s in range(TS):
                            last = pe.transpose(banks[g][:, s * P:(s + 1) * P], n_b[p][:, s, g * P:(g + 1) * P],
                                                eye_sb[:])
                        last.then_inc(p1_tr, 1)
                    pe.wait_ge(p1_cp, c * G + G)
                    for s in range(TS):
                        for k in range(G):
                            last = pe.matmul(banks[0][:, s * E:(s + 1) * E], t_b[p][:, k, s * P:(s + 1) * P],
                                             wa_sb[:, k, :], start=(k == 0), stop=(k == G - 1))
                    last.then_inc(p1_log, 1)
            pe.wait_ge(picked, 1)
            pe.wait_ge(p1_exp, CHUNKS + 2)
            for w, bank in ((tri_sb, hT[0]), (ones_sb, hT[1])):
                pe.matmul(bank[:], w[:], Osum.rearrange("p t e -> p (t e)"), start=True, stop=True)\
                    .then_inc(rank_done, 1)
            pe.wait_ge(slot_done, 1)
            with pe.Fori(0, CHUNKS) as c:
                for src, banks, arrived in ((xn0, hT, (n_in, c * 16 + 16)), (xh1, pre_bank, (norm_done, c + 1))):
                    pe.wait_ge(*arrived)
                    for g in range(G):
                        for s in range(TS):
                            last = pe.transpose(banks[g][:, s * P:(s + 1) * P], src[:, s, g * P:(g + 1) * P], eye_sb[:])
                        last.then_inc(tr_done, 1)
                pe.wait_ge(trc_done, c * (2 * G) + 2 * G)
                for k in range(G):
                    last = pe.matmul(hT[0][:], xpw_sb[:, k, 0:RANK], xnT[:, k, :], start=(k == 0), stop=(k == G - 1))
                last.then_inc(proj_done, 1)
                for k in range(G):
                    last = pe.matmul(hT[1][0:NS, :], xpw_sb[:, k, RANK:RANK + NS], xnT[:, k, :], start=(k == 0),
                                     stop=(k == G - 1))
                last.then_inc(proj_done, 1)
                for s in range(TS):
                    for k in range(G):
                        last = pe.matmul(hT[2][:, s * NS:(s + 1) * NS], xnT[:, k, s * P:(s + 1) * P],
                                         xpw_sb[:, k, RANK + NS:], start=(k == 0), stop=(k == G - 1))
                last.then_inc(proj_done, 1)
                pe.wait_ge(projc_done, c * 2 + 1)
                for g in range(G):
                    pe.matmul(pre_bank[g][:], dtw_sb[:, g * P:(g + 1) * P], drT[:], start=True, stop=True)\
                        .then_inc(pre_done, 1)
                pe.wait_ge(wc_done, c + 1)
                pe.wait_ge(relu_done, c * G + 1)
                for s in range(TS):
                    last = pe.transpose(dA[0][0:ITEMS, s * P:(s + 1) * P], Wc[:, s, :], eye_sb[:])
                last.then_inc(wt_done, 1)
                pe.wait_ge(wtc_done, c + 1)
                pe.wait_ge(cc_done, c + 1)
                pe.wait_ge(projc_done, c * 2 + 2)
                for s in range(TS):
                    pe.matmul(hT[s][:], WT[:, s * P:(s + 1) * P], eb2_sb[:], start=True, stop=True)\
                        .then_inc(bias_done, 1)
                pe.wait_ge(facc_done, c * TS + TS)
                wait_alone(pe, relu_done, c * G + G)

                def shared_part(i, kind, j, half):
                    use = c * USES + BPC + i
                    bank = FP[j % 2]
                    if kind == "down":
                        if j == 0:
                            pe.wait_ge(wd_in, use * 16 + 16)
                            pe.wait_ge(hid_done, (c * SH + i) * FT + FT)
                        elif j >= 2:
                            pe.wait_ge(comb_done, (c * SH + i) * TS + (j - 1) + HEAD)
                        for q in range(FT):
                            last = pe.matmul(bank[:], hid[:, q, j * P:(j + 1) * P], wd[:, q, :],
                                             start=(q == 0), stop=(q == FT - 1))
                        last.then_inc(ffn_done, 1)
                        return
                    if half == 0:
                        if kind == "gate":
                            if j == 0:
                                pe.wait_ge(gu_in, use * 32 + 32)
                            pe.wait_ge(comb_done, (c * SH + i) * TS - FT + j + 1 + HEAD)
                            pe.wait_ge(blk_act, (c + 1) * (BPC * 3) + 1)
                        else:
                            pe.wait_ge(gelu_done, (c * SH + i) * FT + j + 1)
                    gu = 0 if kind == "gate" else 1
                    for q in range(half * G // 2, (half + 1) * G // 2):
                        last = pe.matmul(bank[:], wgu[:, q, gu, j * P:(j + 1) * P], x0T[:, q, :],
                                         start=(q == 0), stop=(q == G - 1))
                    if half == 1:
                        last.then_inc(ffn_done, 1)

                def block_part(i, what):
                    v = c * BPC + i
                    use = c * USES + i
                    if what == "tokens":
                        pe.wait_ge(xg_in, v * 16 + 16)
                        pe.wait_ge(blk_dve, v * 2 + 1)
                        for k in range(G):
                            last = pe.transpose(FP[0][:, k * P:(k + 1) * P], xg[:, k * P:(k + 1) * P], eye_sb[:])
                        last.then_inc(blk_pe, 1)
                    elif what == "gate_up":
                        pe.wait_ge(gu_in, use * 32 + 32)
                        pe.wait_ge(blk_act, v * 3 + 2)
                        for k in range(G):
                            pe.matmul(FP[1][:], xgT[:, k, :], wgu[:, k, :, :].rearrange("p g f -> p (g f)"),
                                      start=(k == 0), stop=False)
                        pe.matmul(FP[1][:], ones_sb[0:1, :], brow[0:1, :], start=False, stop=True).then_inc(blk_pe, 1)
                    elif what == "hidden":
                        pe.wait_ge(blk_dve, v * 2 + 2)
                        for f in range(FT):
                            last = pe.transpose(FP[0][:, f * P:(f + 1) * P], hidr[:, f * P:(f + 1) * P], eye_sb[:])
                        last.then_inc(blk_pe, 1)
                    else:
                        pe.wait_ge(wd_in, use * 16 + 16)
                        pe.wait_ge(blk_dve, v * 2 + 3)
                        for f in range(FT):
                            last = pe.matmul(FP[1][:], hidrT[:, f, :], wd[:, f, :], start=(f == 0), stop=(f == FT - 1))
                        last.then_inc(blk_pe, 1)

                def body(i, kind=None):
                    for k in range(NPI):
                        pe.wait_ge(scan_done, c * UNITS + i * (NPI * G) + (k * G + G + HEAD))
                        for s in range(TS):
                            pe.wait_ge(y_done, c * (NS * TS) + i * (NPI * TS) + (k * TS + s + 1 - TS + HEAD))
                            for g in range(G):
                                last = pe.transpose(hT[s][:, g * P:(g + 1) * P], h[:, k % 2, g, s * P:(s + 1) * P],
                                                    eye_sb[:])
                            last.then_inc(hT_done, 1)
                            if kind == "routed" and k * TS + s in ROUTED:
                                block_part(i, ROUTED[k * TS + s])
                            if kind == "shared" and k * TS + s in SHARED:
                                shared_part(i - ITERS + SH, *SHARED[k * TS + s])

                with pe.Fori(0, BPC) as i:
                    body(i, "routed")
                with pe.Fori(BPC, ITERS - SH) as i:
                    body(i)
                for i in range(ITERS - SH, ITERS):
                    body(i, "shared")
                pe.wait_ge(y_done, (c + 1) * (NS * TS) + HEAD)
                for g in range(G):
                    for s in range(TS):
                        last = pe.transpose(hT[g][:, s * P:(s + 1) * P], yacc[:, s, g * P:(g + 1) * P], eye_sb[:])
                    last.then_inc(yT_done, 1)
                pe.wait_ge(z_done, c * G + G)
                pe.wait_ge(comb_done, (c + 1) * (SH * TS) + HEAD)
                for s in range(TS):
                    for k in range(G):
                        last = pe.matmul(pre_bank[s][:], xnT[:, k, s * P:(s + 1) * P], ow_sb[:, k, :],
                                         start=(k == 0), stop=(k == G - 1))
                    last.then_inc(s_done, 1)


def kernel(**inputs):
    import numpy as np
    import concourse.bacc as bacc
    from concourse.bass_utils import run_bass_kernel_spmd

    v = {k.removeprefix("L0_"): np.asarray(a) for k, a in inputs.items()}

    def tiles(a):
        return a.reshape(-1, P, *a.shape[1:]).swapaxes(0, 1)

    def both(r, s):
        return np.concatenate([v["ffn_" + r], v["ffn_" + s]], 0)

    def by_k(w):
        return w.reshape(ITEMS, -1, P, w.shape[2]).swapaxes(1, 2)

    gate_up = np.stack([by_k(both("rg", "sg")), by_k(both("rw1", "sw1"))], 3).reshape(ITEMS, P, -1)
    down = by_k(both("rw2", "sw2")).reshape(ITEMS, P, -1)
    use_expert = np.zeros((1, CHUNKS * (BPC + 1) + 1), np.float32)
    use_expert[0, BPC:-1:BPC + 1] = E
    mask = np.ones((P, E, TILES), np.float32)
    mask[:, :, 0] = 0
    arrays = {
        "x": v["attn_x"].reshape(-1, DIM),
        "xpw": tiles(v["attn_x_proj_w"].T),
        "dtw": v["attn_dt_proj_w"].T,
        "wa": tiles(v["ffn_wa"]),
        "ow": tiles(v["attn_out_proj_w"].T),
        "cols": np.stack([v["attn_norm_w"], v["attn_norm_b"], v["attn_dt_proj_b"], v["attn_D_param"]])
        .reshape(4, G, P).transpose(2, 0, 1),
        "a_log": tiles(v["attn_A_log"]),
        "ew": np.concatenate([gate_up, down], 2),
        "eb": np.stack([v["ffn_sgb"], v["ffn_sb1"]]).reshape(2, SH, FT, P).transpose(3, 0, 1, 2),
        "ebr": np.concatenate([both("rgb", "sgb"), both("rb1", "sb1")], 1),
        "eb2": both("rb2", "sb2"),
        "eye": np.eye(P, dtype=np.float32),
        "tri": np.triu(np.ones((P, P), np.float32), 1),
        "iota": np.tile(np.arange(E, dtype=np.float32), (P, 1)),
        "mask": mask,
        "bidx": np.repeat(np.arange(BLOCKS, dtype=np.float32), E).reshape(1, BLOCKS, E),
        "be0": use_expert,
        "tokid": np.arange(BATCH * SEQ, dtype=np.uint32).reshape(TILES, P).T,
    }
    arrays = {"in_" + k: np.ascontiguousarray(a) for k, a in arrays.items()}
    nc = bacc.Bacc("TRN2", target_bir_lowering=False, num_devices=1)
    args = [nc.dram_tensor(k, a.shape, mybir.dt.from_np(a.dtype), kind="ExternalInput").ap() for k, a in arrays.items()]
    args.append(nc.dram_tensor("out", [BATCH * SEQ, DIM], F32, kind="ExternalOutput").ap())
    build(nc, *args)
    r = run_bass_kernel_spmd(nc, [arrays], core_ids=[0])
    return r.results[0]["out"].reshape(BATCH, SEQ, DIM)
```

```python
from contextlib import ExitStack

import concourse.bass as bass
from concourse import mybir

F32 = mybir.dt.float32
U32 = mybir.dt.uint32
ALU = mybir.AluOpType
ACT = mybir.ActivationFunctionType
AX = mybir.AxisListType.X

P = 128
DIM = 512
G = DIM // P
T = 512
TS = T // P
BATCH, SEQ = 2, 2048
CPB = SEQ // T
YT = TS - 1
CHUNKS = BATCH * CPB
TILES = CHUNKS * TS
NS = 64
RANK = 128
E, SH, F, TOPK = 16, 2, 256, 2
ITEMS = E + SH
FT = F // P
NPI = 4
ITERS = NS // NPI
BPC = 10
BLOCKS = BPC * CHUNKS
assert RANK == 2 * NS == P
assert BLOCKS >= TOPK * TILES + E - 1 and BPC + SH <= ITERS
USES = BPC + SH
EPS = 1e-5
UNITS = NS * G
HEAD = 4
FFN = 2 * FT + TS

KINDS = {BPC: "y", BPC + 1: "s", BPC + 2: "x", BPC + 3: "shared0", BPC + 4: "shared1", BPC + 5: "shared2"}
assert len(KINDS) == ITERS - BPC
UP0, UP1 = [("up", 0, q) for q in range(G)], [("up", 1, q) for q in range(G)]
GATES = [("gate", f, q) for f in range(FT) for q in range(G)]
SLOTS = {
    "routed": {2: ["tokens"], 3: ["biases"], 4: [0], 5: [1], 7: [2], 9: [3], 12: ["hidden"],
               13: ["down0", "down1"]},
    "y": {4: [0], 5: [1], 8: [2], 9: [3], 13: [(0, 0)], 14: [(0, 1)], 15: [(0, 2)]},
    "s": {**{t: [((3 + t) // G, (3 + t) % G)] for t in range(3 * G + 1)}, 13: ["x0"], 15: ["x1"]},
    "x": {0: ["x2"], 1: ["x3"], 4: ["w"], 8: [0], 9: [1], 12: [2], 13: [3]},
    "shared0": {**{t: [(0, a)] for t, a in enumerate(GATES)},
                **{9 + t: [(0, a)] for t, a in enumerate((UP0 + UP1)[:7])}},
    "shared1": {0: [(0, UP1[-1])], 2: [(0, ("down", 0, 0)), (0, ("down", 0, 1))], 3: [(0, ("down", 1, 0))],
                4: [(0, ("down", 1, 1))], 5: [(0, ("down", 2, 0))], 6: [(0, ("down", 2, 1))],
                7: [(0, ("down", 3, 0)), (0, ("down", 3, 1))], **{8 + t: [(1, a)] for t, a in enumerate(GATES)}},
    "shared2": {**{1 + t: [(1, a)] for t, a in enumerate(UP0 + UP1[:2])}, 7: [(1, UP1[2]), (1, UP1[3])],
                10: [(1, ("down", 0, 0)), (1, ("down", 0, 1))], 11: [(1, ("down", 1, 0))], 12: [(1, ("down", 1, 1))],
                13: [(1, ("down", 2, 0)), (1, ("down", 2, 1))], 14: [(1, ("down", 3, 0)), (1, ("down", 3, 1))]},
}
EXTRAS = {
    ("y", 2, 1): [("z", (0,))], ("y", 2, 2): [("z", (1,))], ("y", 3, 1): [("z", (2,))], ("y", 3, 2): [("z", (3,))],
    ("x", 3, 1): [("seed", (0,))], ("x", 3, 2): [("seed", (1,))],
    ("x", 0, 1): [("seed", (2,))], ("x", 0, 2): [("seed", (3,))],
    ("shared0", 0, 3): [("hidden", (0, 0))],
    ("shared1", 1, 0): [("hidden", (0, 1))], ("shared1", 1, 3): [("combine", (0, 0))],
    ("shared1", 2, 1): [("combine", (0, 1))], ("shared1", 2, 3): [("combine", (0, 2))],
    ("shared1", 3, 1): [("combine", (0, 3))],
    ("shared2", 2, 1): [("hidden", (1, 0))], ("shared2", 3, 0): [("hidden", (1, 1))],
    ("shared2", 3, 3): [("combine", (1, 0))], ("shared2", 0, 1): [("combine", (1, 1))],
    ("shared2", 0, 3): [("combine", (1, 2)), ("combine", (1, 3))],
}


def build(nc, x, xpw, dtw, wa, ow, cols, a_log, ew, eb, ebr, eb2, eye, tri, iota, mask, bidx, be0, ctab, tokid, out):
    x_v = x.rearrange("(c s p) d -> c p s d", s=TS, p=P)
    out_v = out.rearrange("(c s p) d -> c p s d", s=TS, p=P)

    def dram(name, shape, dt=F32):
        return nc.dram_tensor(name, shape, dt, kind="Internal").ap()

    xn_dram = dram("xn_scratch", [BATCH * SEQ, DIM])
    s_dram = dram("s_scratch", [BATCH * SEQ + T, DIM])
    d_dram = dram("d_scratch", [CHUNKS, P, G, T])
    u_dram = dram("u_scratch", [CHUNKS, P, G, T])
    f_dram = dram("f_scratch", [BATCH * SEQ + T, DIM])
    y_dram = dram("y_scratch", [BLOCKS * P, DIM])
    bt_dram = dram("bt_scratch", [CHUNKS * NS + NPI, T])
    by_chunk = "(c s p) d -> c p s d"
    xn_v, s_v, f_v = (a.rearrange(by_chunk, s=TS, p=P) for a in (xn_dram, s_dram, f_dram))

    with ExitStack() as ctx:
        def sb(name, shape, dt=F32):
            return ctx.enter_context(nc.sbuf_tensor(name, shape, dt))

        def sem(name):
            return ctx.enter_context(nc.semaphore(name))

        xpw_sb = sb("xpw_sb", [P, G, RANK + 2 * NS])
        dtw_sb = sb("dtw_sb", [P, DIM])
        wa_sb = sb("wa_sb", [P, G, E])
        ow_sb = sb("ow_sb", [P, G, DIM])
        cols_sb = sb("cols_sb", [P, 4, G])
        nw, nb, dtb, dpar = (cols_sb[:, i, :] for i in range(4))
        A = sb("A", [P, G, NS])
        eb_sb = sb("eb_sb", [P, 2, SH, FT])
        eb2_sb = sb("eb2_sb", [ITEMS, DIM])
        eye_sb = sb("eye_sb", [P, P])
        tri_sb = sb("tri_sb", [P, P])
        ones_sb = sb("ones_sb", [P, P])
        iota_sb = sb("iota_sb", [P, P])
        mask_sb = sb("mask_sb", [P, E, TILES])
        bidx_sb = sb("bidx_sb", [1, BLOCKS, E])
        be0_sb = sb("be0_sb", [1, CHUNKS * (BPC + 1) + 1])
        ctab_sb = sb("ctab_sb", [1, CHUNKS + 1, 3], U32)
        tokid_sb = sb("tokid_sb", [P, TILES])
        consts = ((xpw_sb, xpw), (dtw_sb, dtw), (wa_sb, wa), (ow_sb, ow), (cols_sb, cols), (A, a_log), (eb_sb, eb),
                  (eb2_sb, eb2), (eye_sb, eye), (tri_sb, tri), (iota_sb, iota), (mask_sb, mask), (bidx_sb, bidx),
                  (be0_sb, be0), (ctab_sb, ctab), (tokid_sb, tokid))
        nhalf = sb("nhalf", [P, TS])
        wgu = sb("wgu", [P, G, 2, F])
        wd = sb("wd", [P, FT, DIM])
        brow = sb("brow", [1, 2 * F])
        xn0 = sb("xn0", [P, TS, DIM])
        s_sb = sb("s_sb", [P, TS, DIM])
        x0T = sb("x0T", [P, G, T])
        zT = sb("zT", [P, G, T])
        stats = sb("stats", [P, TS, 6])
        mv = sb("mv", [P, TS, 2])
        veps = sb("veps", [P, TS])
        rstd = sb("rstd", [P, TS])
        drT = sb("drT", [P, T])
        bcT = sb("bcT", [2 * NS, T])
        cc = sb("cc", [P, TILES, NS])
        sp = sb("sp", [P, G, T])
        spl = sb("spl", [P, G, T])
        facc = sb("facc", [P, TS, DIM])
        yacc = sb("yacc", [P, 2 * TS, DIM])
        ch = sb("ch", [P, DIM])
        yprev = sb("yprev", [P, TS, DIM])
        zero = sb("zero", [P, DIM])
        state = sb("state", [P, G, 2 * NS])
        h = sb("h", [P, 2, G, T])
        dbx = sb("dbx", [P, G, T])
        bbc = sb("bbc", [P, NPI, T])
        hg = sb("hg", [P, FT, T])
        hid = sb("hid", [P, FT, T])
        aff = sb("aff", [P, TILES, E])
        top = sb("top", [P, TOPK, TILES])
        pick = sb("pick", [P, TOPK, TILES])
        rsum = sb("rsum", [P, TILES])
        W = sb("W", [P, TILES, ITEMS])
        Wc = sb("Wc", [P, TS, ITEMS])
        WT = sb("WT", [ITEMS, T])
        per_e = sb("per_e", [P, 4, E])
        per_e_u = sb("per_e_u", [P, E], U32)
        slot_f = sb("slot_f", [P, TOPK, TILES])
        slot_u = sb("slot_u", [P, TOPK, TILES], U32)
        part_u = sb("part_u", [P, 2, TOPK, TILES], U32)
        part_f = sb("part_f", [P, 2, TOPK, TILES])
        be_u = sb("be_u", [1, CHUNKS * (BPC + 1) + 1], U32)
        tok_sb = sb("tok_sb", [P, BLOCKS + 1], U32)
        idx = sb("idx", [P, 1], U32)
        xg = sb("xg", [P, DIM])
        xgT = sb("xgT", [P, G, P])
        hgr = sb("hgr", [P, F])
        hidr = sb("hidr", [P, F])
        hidrT = sb("hidrT", [P, FT, P])
        yo = sb("yo", [P, DIM])
        x_b = (h[:, 0], h[:, 1])
        n_b = (xn0, facc)
        h_b = (s_sb, yacc[:, 0:TS])
        t_b = (zT, yprev)
        sp_b = (sp, dbx)
        spl_b = (spl, bbc)
        x4, s4, f4, r4 = (xn0, s_sb), (x0T, zT), (facc, yacc[:, 0:TS]), ((sp, spl), (h[:, 0], h[:, 1]))
        idx4 = sb("idx4", [P, 2, TOPK, TS], U32)
        eq, cand, aff2, pos = (dbx[:, i, :].rearrange("p (t e) -> p t e", e=E) for i in range(4))
        O = [bbc[:, j, :].rearrange("p (t e) -> p t e", e=E) for j in range(TOPK)]
        Osum, Wtmp = (bbc[:, j, :].rearrange("p (t e) -> p t e", e=E) for j in (2, 3))
        cnt, cum, excl = (a.rearrange("p (e t) -> p e t", e=E) for a in (hg[:, 0, :], hg[:, 1, :], hid[:, 0, :]))
        rows = [a[:].rearrange(r).rearrange("p (t r) -> p t r", r=P)
                for a, r in ((h, "p a b c -> p (a b c)"), (yacc, "p a b -> p (a b)"))]
        cols_at = [[a[:].rearrange("p a b -> p (a b)")[:, 0:TILES // 2 * (BLOCKS + 1)]
                    .rearrange("p (t b) -> p t b", b=BLOCKS + 1) for a in pair] for pair in ((x0T, s_sb), (zT, yprev))]
        bcmp = h[0:1, 0].rearrange("p a b -> p (a b)")[:, 0:BLOCKS * E].rearrange("p (b e) -> p b e", e=E)

        hT = [ctx.enter_context(nc.psum_tensor(f"hT{i}", [P, 512], F32)) for i in range(TS)]
        dA = [ctx.enter_context(nc.psum_tensor(f"dA{i}", [P, 512], F32)) for i in range(2)]
        FP = [ctx.enter_context(nc.psum_tensor(f"FP{i}", [P, 512], F32)) for i in range(2)]
        y_bank = hT[TS - 1]
        pre_bank = [dA[0], dA[1], FP[0], FP[1]]
        x_bank = [hT[2], hT[0], hT[1], hT[3]]

        const_in = sem("const_in")
        dve_const = sem("dve_const")
        passed = sem("passed")
        a_exp = sem("a_exp")
        x_in = [sem(f"x_in{i}") for i in range(2)]
        p1_out = [sem(f"p1_out{i}") for i in range(2)]
        du_out = [sem(f"du_out{i}") for i in range(2)]
        bt_out = sem("bt_out")
        p1_bn = sem("p1_bn")
        p1_stats = sem("p1_stats")
        p1_add = sem("p1_add")
        p1_rstd = sem("p1_rstd")
        p1_norm = sem("p1_norm")
        p1_tr = sem("p1_tr")
        p1_cp = sem("p1_cp")
        p1_pe = sem("p1_pe")
        p1_act = sem("p1_act")
        cc_done = sem("cc_done")
        pre_done = sem("pre_done")
        abs_done = sem("abs_done")
        relu_done = sem("relu_done")
        spe_done = sem("spe_done")
        ln_done = sem("ln_done")
        delta_done = sem("delta_done")
        u_done = sem("u_done")
        r_link = sem("r_link")
        picked = sem("picked")
        rank_done = sem("rank_done")
        row_done = sem("row_done")
        col_done = sem("col_done")
        tok_pe = sem("tok_pe")
        tok_done = sem("tok_done")
        be_done = sem("be_done")
        b_in = [sem(f"b_in{i}") for i in range(NPI)]
        d_in = [sem(f"d_in{i}") for i in range(G)]
        u_in = [sem(f"u_in{i}") for i in range(G)]
        n_in = sem("n_in")
        cleared = sem("cleared")
        exp_done = sem("exp_done")
        dbx_done = sem("dbx_done")
        scan_done = sem("scan_done")
        hT_done = sem("hT_done")
        hL_done = sem("hL_done")
        ch_done = sem("ch_done")
        yL_done = sem("yL_done")
        y_clear = sem("y_clear")
        y_done = sem("y_done")
        state_done = sem("state_done")
        ycopy_done = sem("ycopy_done")
        yzero_done = sem("yzero_done")
        yT_done = sem("yT_done")
        z_done = sem("z_done")
        s_done = sem("s_done")
        sc_done = sem("sc_done")
        xT_done = sem("xT_done")
        xTc_done = sem("xTc_done")
        wc_done = sem("wc_done")
        wt_done = sem("wt_done")
        wtc_done = sem("wtc_done")
        bias_done = sem("bias_done")
        facc_done = sem("facc_done")
        f_out, s_out = sem("f_out"), sem("s_out")
        gu_in, wd_in = sem("gu_in"), sem("wd_in")
        xg_in = sem("xg_in")
        idx_done = sem("idx_done")
        blk_pe = sem("blk_pe")
        blk_act = sem("blk_act")
        blk_dve = sem("blk_dve")
        yo_out = sem("yo_out")
        ffn_done = sem("ffn_done")
        gelu_done = sem("gelu_done")
        hid_done = sem("hid_done")
        comb_done = sem("comb_done")
        in4 = [sem(f"in4_{i}") for i in range(2)]
        idx4_done = sem("idx4_done")
        rows4 = [sem(f"rows4_{i}") for i in range(2)]
        f4_done = sem("f4_done")
        silu_done = sem("silu_done")
        g4_done = sem("g4_done")
        o4_done = sem("o4_done")
        out_dma = [sem(f"out_dma{i}") for i in range(2)]

        block = ctx.enter_context(nc.Block())

        def wait_alone(eng, sem, value):
            eng.wait_ge(sem, value)
            eng.sem_inc(passed, 1)

        @block.sync
        def _(sp):
            for dst, src in consts:
                sp.dma_start(dst[:], src).then_inc(const_in, 16)
            for done in (*p1_out, *du_out, *out_dma, bt_out, f_out, s_out):
                sp.sem_inc(done, HEAD)
            for p in range(2):
                sp.dma_start(x_b[p], x_v[p]).then_inc(x_in[p], 16)

            def store_n(c, p, more=True):
                sp.wait_ge(p1_norm, c * 2 + 1)
                sp.dma_start(xn_v[c], n_b[p][:]).then_inc(p1_out[p], 16)
                if more:
                    sp.dma_start(x_b[p], x_v[c + 2]).then_inc(x_in[p], 16)

            def store_b(c):
                sp.wait_ge(p1_act, c * 3 + 6)
                sp.dma_start(bt_dram[bass.ds(c * NS, NS), :], bcT[0:NS, :]).then_inc(bt_out, 16)

            def store_du(c, p):
                sp.wait_ge(delta_done, c + 1)
                sp.dma_start(d_dram[c], sp_b[p][:]).then_inc(du_out[p], 16)
                sp.wait_ge(u_done, c + 1)
                sp.dma_start(u_dram[c], spl_b[p][:]).then_inc(du_out[p], 16)

            store_n(0, 0)
            with sp.Fori(0, CHUNKS // 2 - 2) as cp:
                for p in range(2):
                    store_b(cp * 2 + p)
                    store_n(cp * 2 + (p + 1), 1 - p)
                    store_du(cp * 2 + p, p)
            for c in range(CHUNKS - 4, CHUNKS - 1):
                store_b(c)
                store_n(c + 1, (c + 1) % 2, c + 3 < CHUNKS)
                store_du(c, c % 2)
            store_b(CHUNKS - 1)
            sp.dma_start(bt_dram[CHUNKS * NS:, :], bcT[0:NPI, :]).then_inc(bt_out, 16)
            store_du(CHUNKS - 1, 1)
            def expert(use):
                return sp.value_load(be_u[0:1, bass.ds(use, 1)], min_val=0, max_val=ITEMS - 1)

            def load_gu(i):
                sp.dma_start(wgu[:], ew[bass.ds(i, 1), :, 0:2 * G * F].rearrange("o p (k g f) -> (o p) k g f", k=G, g=2))\
                    .then_inc(gu_in, 16)
                sp.dma_start(brow[:], ebr[bass.ds(i, 1), :]).then_inc(gu_in, 16)

            def load_wd(i):
                sp.dma_start(wd[:], ew[bass.ds(i, 1), :, 2 * G * F:].rearrange("o p (k d) -> (o p) k d", k=FT))\
                    .then_inc(wd_in, 16)

            def load_b(row, j):
                sp.dma_start(bbc[:, j, :], bt_dram[row, :].partition_broadcast(P)).then_inc(b_in[j], 16)

            def load_u(c, g):
                sp.dma_start(spl[:, g, :], u_dram[c, :, g, :]).then_inc(u_in[g], 16)

            def load_d(c, g):
                sp.dma_start(sp_b[0][:, g, :], d_dram[c, :, g, :]).then_inc(d_in[g], 16)

            for p in range(2):
                sp.wait_ge(p1_out[p], CHUNKS // 2 * 16 + HEAD)
                sp.wait_ge(du_out[p], CHUNKS * 16 + HEAD)
            sp.wait_ge(bt_out, CHUNKS * 16 + 16 + HEAD)
            for g in range(G):
                load_u(0, g)
                load_d(0, g)

            sp.wait_ge(be_done, 1)
            load_gu(expert(0))
            sp.wait_ge(cleared, 1)
            for j in range(NPI):
                load_b(j, j)

            def body(c, i, kind=None, last=False, next_c=None):
                if kind == "y":
                    sp.wait_ge(facc_done, c * TS + HEAD)
                    sp.dma_start(xn0[:], xn_v[c]).then_inc(n_in, 16)
                for k in range(NPI):
                    done = c * UNITS + i * (NPI * G) + k * G
                    if last and k == NPI - 1:
                        for g in range(G):
                            sp.wait_ge(dbx_done, done + g + 1)
                            load_u(next_c, g)
                            sp.wait_ge(exp_done, done + g + 1)
                            load_d(next_c, g)
                    sp.wait_ge(dbx_done, done + G)
                    load_b(c * NS + i * NPI + (NPI + k), k)
                    if kind == "routed":
                        block = c * BPC + i
                        if k == 1:
                            sp.wait_ge(ffn_done, c * (SH * FFN) + 1)
                            sp.wait_ge(blk_pe, block * 4 + 1)
                            load_wd(expert(c * (BPC + 1) + i))
                        if k == 2:
                            sp.wait_ge(blk_pe, block * 4 + 3)
                            load_gu(expert(c * (BPC + 1) + i + 1))
                        if k == 3:
                            sp.wait_ge(blk_dve, block * 2 + 3)
                            sp.dma_start(y_dram[bass.ds(block * P, P), :], yo[:]).then_inc(yo_out, 16)
                    if kind == "y" and k == 0:
                        sp.wait_ge(comb_done, c * (SH * TS) + HEAD)
                        sp.dma_start(f_v[c], facc[:]).then_inc(f_out, 16)
                    if kind == "y" and k == 1:
                        sp.wait_ge(blk_pe, (c + 1) * (BPC * 4) + 1)
                        load_wd(E)
                    if kind == "x" and k == 1:
                        sp.wait_ge(sc_done, c * TS + TS + HEAD)
                        sp.dma_start(s_v[c], s_sb[:]).then_inc(s_out, 16)
                    if kind == "shared1" and k == 2:
                        sp.wait_ge(ffn_done, c * (SH * FFN) + 2 * FT + 1)
                        load_gu(E + 1)
                    if kind == "shared1" and k == 3:
                        sp.wait_ge(ffn_done, c * (SH * FFN) + FFN + 1)
                        load_wd(E + 1)
                    if last and k == NPI - 1:
                        sp.wait_ge(ffn_done, c * (SH * FFN) + FFN + 2 * FT + 1)
                        load_gu(expert((c + 1) * (BPC + 1)))

            def chunk(c, next_c):
                with sp.Fori(0, BPC) as i:
                    body(c, i, "routed")
                for i, kind in KINDS.items():
                    body(c, i, kind, i == ITERS - 1, next_c)

            with sp.Fori(0, CHUNKS - 1) as c:
                chunk(c, c + 1)
            chunk(CHUNKS - 1, CHUNKS - 1)
            sp.wait_ge(comb_done, CHUNKS * (SH * TS) + HEAD)
            sp.dma_start(f_v[CHUNKS], facc[:]).then_inc(f_out, 16)

            def load_x(c, p):
                sp.dma_start(x4[p][:], x_v[c]).then_inc(in4[p], 16)

            def load_s(c, p):
                sp.dma_start(s4[p][:], s_v[c + 1]).then_inc(in4[p], 16)

            def load_f(c, p):
                sp.dma_start(f4[p][:], f_v[c + 1]).then_inc(in4[p], 16)

            sp.wait_ge(facc_done, CHUNKS * TS + HEAD)
            load_x(0, 0)
            sp.wait_ge(f_out, (CHUNKS + 1) * 16 + HEAD)
            load_f(0, 0)
            sp.wait_ge(z_done, (CHUNKS + 1) * G + HEAD)
            load_s(0, 0)
            sp.wait_ge(y_done, CHUNKS * NS * YT + HEAD)
            sp.wait_ge(ycopy_done, CHUNKS * TS + YT)
            load_f(1, 1)
            sp.wait_ge(sc_done, (CHUNKS + 1) * TS + HEAD)
            sp.dma_start(s_v[CHUNKS], s_sb[:]).then_inc(s_out, 16)
            load_s(1, 1)
            sp.wait_ge(s_out, (CHUNKS + 1) * 16 + HEAD)
            load_x(1, 1)

            def load4(c, p):
                load_x(c, p)
                load_s(c, p)
                load_f(c, p)

            def phase4(c, cp, p, more=True):
                sp.wait_ge(o4_done, c + 3)
                sp.dma_start(out_v[c], x4[p][:]).then_inc(out_dma[p], 16)
                if more:
                    sp.wait_ge(out_dma[p], cp * 16 + 16 + HEAD)
                    load4(c + 2, p)

            with sp.Fori(0, CHUNKS // 2 - 1) as cp:
                for p in range(2):
                    phase4(cp * 2 + p, cp, p)
            for p in range(2):
                phase4(CHUNKS - 2 + p, CHUNKS // 2 - 1, p, False)
            for p in range(2):
                sp.wait_ge(out_dma[p], CHUNKS // 2 * 16 + HEAD)
            sp.wait_ge(yo_out, BLOCKS * 16 + HEAD)
            for g in range(G):
                sp.wait_ge(u_in[g], (CHUNKS + 1) * 16)
                sp.wait_ge(d_in[g], (CHUNKS + 1) * 16)
            for j in range(NPI):
                sp.wait_ge(b_in[j], (CHUNKS * ITERS + 1) * 16)
            sp.wait_ge(xg_in, BLOCKS * 16 + 16)
            sp.wait_ge(gu_in, CHUNKS * USES * 32 + 32)

        @block.gpsimd
        def _(pool):
            pool.wait_ge(dve_const, 1)

            with pool.Fori(0, CHUNKS * 2) as r:
                wait_alone(pool, p1_stats, r + 1)
                pool.tensor_scalar(veps[:], mv[:, :, 1], EPS, None, ALU.add).then_inc(p1_add, 1)
                pool.wait_ge(p1_add, r + 1)
                pool.tensor_tensor(rstd[:], veps[:], nhalf[:], ALU.pow).then_inc(p1_rstd, 1)

            def gather(v):
                pool.tensor_copy(idx[:], tok_sb[:, bass.ds(v, 1)]).then_inc(idx_done, 1)
                wait_alone(pool, idx_done, v + 1)
                pool.indirect_dma_start(xg[:], None, xn_dram, bass.IndirectOffsetOnAxis(idx[:, 0:1], 0))\
                    .then_inc(xg_in, 16)

            pool.wait_ge(tok_done, 1)
            for p in range(2):
                pool.wait_ge(p1_out[p], CHUNKS // 2 * 16 + HEAD)
            gather(0)
            with pool.Fori(0, CHUNKS) as c:

                def body(i, routed=False):
                    for k in range(NPI):
                        pool.wait_ge(b_in[k], c * (ITERS * 16) + i * 16 + 16)
                        for g in range(G):
                            if k == 0:
                                pool.wait_ge(u_in[g], c * 16 + 16)
                            pool.wait_ge(scan_done, c * UNITS + i * (NPI * G) + (k * G + g - G + 1) + HEAD)
                            pool.tensor_tensor(dbx[:, g, :], spl[:, g, :], bbc[:, k, :], ALU.mult)\
                                .then_inc(dbx_done, 1)
                        if routed and k == 2:
                            wait_alone(pool, blk_pe, (c * BPC + i) * 4 + 2)
                            gather(c * BPC + i + 1)

                with pool.Fori(0, BPC) as i:
                    body(i, True)
                with pool.Fori(BPC, ITERS) as i:
                    body(i)
            pool.wait_ge(b_in[0], CHUNKS * (ITERS * 16) + 16)
            for g in range(G):
                pool.wait_ge(u_in[g], CHUNKS * 16 + 16)
                pool.wait_ge(scan_done, CHUNKS * UNITS + (g - G + 1) + HEAD)
                pool.tensor_tensor(dbx[:, g, :], spl[:, g, :], bbc[:, 0, :], ALU.mult).then_inc(dbx_done, 1)

            pool.wait_ge(yo_out, BLOCKS * 16 + HEAD)
            pool.wait_ge(scan_done, CHUNKS * UNITS + G + HEAD)
            pool.wait_ge(state_done, CHUNKS * NS + HEAD)
            pool.wait_ge(hT_done, CHUNKS * NS * YT)
            pool.wait_ge(hL_done, CHUNKS * NS)
            with pool.Fori(0, CHUNKS // 2) as cp:
                for p in range(2):
                    c = cp * 2 + p
                    wait_alone(pool, o4_done, c + 1)
                    for j in range(TOPK):
                        last = pool.tensor_copy(idx4[:, p, j, :], slot_u[:, j, bass.ds(c * TS, TS)])
                    last.then_inc(idx4_done, 1)
                    wait_alone(pool, idx4_done, c + 1)
                    for s in range(TS):
                        for j in range(TOPK):
                            pool.indirect_dma_start(r4[p][j][:, s, :], None, y_dram,
                                                    bass.IndirectOffsetOnAxis(idx4[:, p, j, s:s + 1], 0))\
                                .then_inc(rows4[p], 16)

        @block.scalar
        def _(act):
            act.wait_ge(const_in, 16 * len(consts))
            act.activation(A[:], A[:], ACT.Exp).then_inc(a_exp, 1)
            for done, n in ((p1_act, 3), (blk_act, 1), (yo_out, HEAD), (sc_done, HEAD), (yzero_done, HEAD), (relu_done, G),
                            (state_done, HEAD)):
                act.sem_inc(done, n)

            def transposed(c, p, used=None):
                for g in range(G):
                    act.wait_ge(p1_tr, c * (2 * G) + (g + 1 + 2 * G))
                    act.activation(x0T[:, g, :], x_bank[g][:], ACT.Copy).then_inc(p1_cp, 1)
                if used is not None:
                    act.wait_ge(u_done, used)
                for g in range(G):
                    act.wait_ge(p1_tr, c * (2 * G) + (G + g + 1 + 2 * G))
                    act.activation(t_b[p][:, g, :], pre_bank[g][:], ACT.Identity, scale=nw[:, g:g + 1],
                                   bias=nb[:, g:g + 1]).then_inc(p1_cp, 1)

            def projected(c, p):
                act.wait_ge(p1_pe, c * 4 + 1)
                act.activation(aff[:, bass.ds(c * TS, TS), :], hT[3][:, 0:TS * E].rearrange("p (s e) -> p s e", s=TS),
                               ACT.Exp, scale=-1.0).then_inc(p1_act, 1)
                act.wait_ge(p1_pe, c * 4 + 2)
                act.activation(drT[:], hT[0][:], ACT.Copy).then_inc(p1_act, 1)
                act.wait_ge(p1_pe, c * 4 + 3)
                act.wait_ge(bt_out, c * 16 + HEAD)
                act.activation(bcT[:], hT[1][:], ACT.Copy).then_inc(p1_act, 1)
                act.wait_ge(du_out[p], (c - p) * 16 + HEAD)
                for g in range(G):
                    act.wait_ge(pre_done, c * G + g + 1)
                    act.activation(spl_b[p][:, g, :], pre_bank[g][:], ACT.Abs, bias=dtb[:, g:g + 1])\
                        .then_inc(abs_done, 1)
                    act.activation(sp_b[p][:, g, :], pre_bank[g][:], ACT.Relu, bias=dtb[:, g:g + 1])\
                        .then_inc(relu_done, 1)

            def softplus(c, p):
                act.wait_ge(abs_done, c * G + G)
                act.activation(spl_b[p][:], spl_b[p][:], ACT.Exp, scale=-1.0).then_inc(spe_done, 1)
                act.wait_ge(spe_done, c + 1)
                act.activation(spl_b[p][:], spl_b[p][:], ACT.Ln, bias=1.0).then_inc(ln_done, 1)

            transposed(0, 0)
            projected(0, 0)
            transposed(1, 1)
            softplus(0, 0)
            with act.Fori(1, CHUNKS - 1, 2) as c:
                projected(c, 1)
                transposed(c + 1, 0, c)
                softplus(c, 1)
                projected(c + 1, 0)
                transposed(c + 2, 1, c + 1)
                softplus(c + 1, 0)
            projected(CHUNKS - 1, 1)
            softplus(CHUNKS - 1, 1)

            act.wait_ge(dve_const, 3)
            act.wait_ge(cleared, 1)

            def step(c, n, k, kind=None, i=None, nxt=0, first=False):
                for g in range(G):
                    if (type(n) is int and n == 0) or nxt:
                        act.wait_ge(d_in[g], (c + nxt) * 16 + 16)
                    act.wait_ge(scan_done, (c + nxt) * UNITS + (0 if nxt else n) * G + (g - 1) + HEAD)
                    act.activation(dA[g % 2][:], sp[:, g, :], ACT.Exp, scale=A[:, g, bass.ds(0 if nxt else n, 1)])\
                        .then_inc(exp_done, 1)
                    if g == 1 and not first:
                        act.activation(state[:, :, bass.ds(n - 1, 1)], h[:, (k + 1) % 2, :, T - 1:T], ACT.Copy)\
                            .then_inc(state_done, 1)
                    if kind == "routed" and (k, g) == (0, 2):
                        act.wait_ge(blk_pe, (c * BPC + i) * 4 + 4)
                        act.activation(hidrT[:], FP[0][:, 0:F].rearrange("p (f t) -> p f t", f=FT), ACT.Copy)\
                            .then_inc(blk_act, 1)
                    if g == 2 and not first:
                        act.wait_ge(hL_done, c * NS + n)
                        act.wait_ge(yL_done, c * NS + n - 1 + HEAD)
                        act.activation(ch[:], hT[YT - 1][:], ACT.Copy,
                                       scale=cc[:, bass.ds(c * TS + YT, 1), bass.ds(n - 1, 1)]).then_inc(ch_done, 1)
                    if nxt and g == 3:
                        act.wait_ge(yT_done, (c + 1) * G + HEAD)
                        act.wait_ge(yL_done, (c + 1) * NS + HEAD)
                        act.activation(yprev[:, YT, :], y_bank[:], ACT.Copy).then_inc(ycopy_done, 1)
                    at = (k, g)
                    if kind == "routed":
                        block = c * BPC + i
                        if at == (1, 3):
                            act.wait_ge(blk_pe, block * 4 + 2)
                            act.activation(xgT[:], FP[0][:].rearrange("p (k t) -> p k t", k=G), ACT.Copy)\
                                .then_inc(blk_act, 1)
                        if at == (3, 3):
                            act.wait_ge(blk_pe, block * 4 + 3)
                            act.activation(hgr[:], FP[1][:, 0:F], ACT.Gelu).then_inc(blk_act, 1)
                    if kind == "y" and k == 1 and g < YT:
                        if g == 0:
                            act.wait_ge(yT_done, c * G + HEAD)
                        act.activation(yprev[:, g, :], yacc[:, bass.ds(half_before + g, 1), :], ACT.Copy)\
                            .then_inc(ycopy_done, 1)
                    if kind == "y" and k == 2 and g < YT:
                        wait_alone(act, ycopy_done, c * TS + g + 1)
                        act.activation(yacc[:, bass.ds(half_before + g, 1), :], zero[:], ACT.Copy).then_inc(yzero_done, 1)
                    if kind == "s" and g == 2:
                        out_copy(c, (k - 1) % NPI)
                    if (kind, *at) == ("s", 0, 3):
                        x_copy(c, 0)
                    if (kind, k) == ("x", 1):
                        if g == 0:
                            act.activation(Wc[:], W[:, bass.ds(c * TS, TS), :], ACT.Copy).then_inc(wc_done, 1)
                        else:
                            x_copy(c, g)
                    if kind == "x" and at == (2, 2):
                        act.wait_ge(wt_done, c + 1)
                        act.activation(WT[:], FP[0][0:ITEMS, :], ACT.Copy).then_inc(wtc_done, 1)
                    if (kind, *at) == ("shared0", 3, 1):
                        gelus(c, 0)
                    if (kind, *at) == ("shared2", 1, 1):
                        gelus(c, 1)

            def x_copy(c, g):
                act.wait_ge(xT_done, c * G + g + 1)
                act.activation(x0T[:, g, :], FP[g % 2][:], ACT.Copy).then_inc(xTc_done, 1)

            def gelus(c, e):
                for f in range(FT):
                    act.wait_ge(ffn_done, (c * SH + e) * FFN + f + 2)
                    act.activation(hg[:, f, :], FP[f][:], ACT.Gelu, bias=eb_sb[:, 0, e, f:f + 1])\
                        .then_inc(gelu_done, 1)

            def out_copy(c, s):
                if s == 0:
                    act.wait_ge(s_out, c * 16 + HEAD)
                act.wait_ge(s_done, c * TS + s + 1)
                act.activation(s_sb[:, s, :], FP[s % 2][:], ACT.Copy).then_inc(sc_done, 1)

            step(0, 0, 0, first=True)
            with act.Fori(0, CHUNKS) as c:
                half_before = act.value_load(ctab_sb[0:1, bass.ds(c, 1), 2], min_val=0, max_val=TS)
                with act.Fori(0, BPC) as i:
                    for k in range(1, NPI + 1):
                        step(c, i * NPI + k, k % NPI, "routed", i)
                for i, kind in KINDS.items():
                    for k in range(1, NPI + 1):
                        step(c, i * NPI + k, k % NPI, kind, i, nxt=int(i * NPI + k == NS))
            half = (CHUNKS - 1) % 2 * TS
            for s in range(YT):
                act.wait_ge(y_done, CHUNKS * NS * YT - YT + s + 1 + HEAD)
                act.activation(yprev[:, s, :], yacc[:, half + s, :], ACT.Copy).then_inc(ycopy_done, 1)
            for s in range(TS):
                out_copy(CHUNKS, s)
            with act.Fori(0, CHUNKS // 2) as cp:
                for p in range(2):
                    act.wait_ge(f4_done, (cp * 2 + p) * TOPK + TOPK)
                    act.activation(f4[p][:], f4[p][:], ACT.Silu).then_inc(silu_done, 1)

        @block.vector
        def _(dve):
            dve.memset(nhalf[:], -0.5).then_inc(dve_const, 1)
            dve.memset(W[:], 1.0)
            dve.memset(ones_sb[:], 1.0)
            dve.memset(per_e[:, 2, :], 1.0).then_inc(dve_const, 1)
            dve.memset(zero[:], 0.0)
            for done, n in ((scan_done, HEAD), (comb_done, HEAD), (y_done, HEAD), (z_done, HEAD), (facc_done, HEAD),
                            (blk_dve, 1), (o4_done, 2), (cc_done, 1)):
                dve.sem_inc(done, n)
            dve.wait_ge(a_exp, 1)
            dve.tensor_scalar(A[:], A[:], -1.0, None, ALU.mult).then_inc(dve_const, 1)
            dve.wait_ge(dve_const, 3)

            def norms(c, p, first=False):
                wait_alone(dve, x_in[p], (c - p) * 8 + 16)
                for r, (src, dst) in enumerate(((x_b[p], n_b[p]), (n_b[p], h_b[p]))):
                    for s in range(TS):
                        last = dve.bn_stats(stats[:, s, :], src[:, s, :])
                    last.then_inc(p1_bn, 1)
                    wait_alone(dve, p1_bn, c * 2 + r + 1)
                    for s in range(TS):
                        last = dve.bn_aggr(mv[:, s, :], stats[:, s, :])
                    last.then_inc(p1_stats, 1)
                    dve.wait_ge(p1_rstd, c * 2 + r + 1)
                    if r == 0:
                        dve.wait_ge(p1_out[p], (c - p) * 8 + HEAD)
                    dve.wait_ge(p1_tr, c * (2 * G) - (G if r == 0 else 0) + G)
                    for s in range(TS):
                        last = dve.tensor_scalar(dst[:, s, :], src[:, s, :], mv[:, s, 0:1], rstd[:, s:s + 1],
                                                 ALU.subtract, ALU.mult)
                    last.then_inc(p1_norm, 1)
                    if r == 0:
                        wait_alone(dve, p1_norm, c * 2 + 1)

            def keep_c(c):
                dve.wait_ge(p1_pe, c * 4 + 4)
                dve.tensor_copy(cc[:, bass.ds(c * TS, TS), :],
                                hT[3][:].rearrange("p (s n) -> p s n", s=TS)[:, :, NS:2 * NS]).then_inc(cc_done, 1)

            def deltas(c, p):
                dve.wait_ge(relu_done, c * G + 2 * G)
                dve.wait_ge(ln_done, c + 1)
                dve.tensor_tensor(sp_b[p][:], sp_b[p][:], spl_b[p][:], ALU.add).then_inc(delta_done, 1)
                dve.wait_ge(delta_done, c + 1)
                dve.tensor_tensor(spl_b[p][:], sp_b[p][:], t_b[p][:], ALU.mult).then_inc(u_done, 1)

            norms(0, 0)
            norms(1, 1)
            keep_c(0)
            with dve.Fori(0, CHUNKS // 2 - 1) as cp:
                norms(cp * 2 + 2, 0)
                deltas(cp * 2, 0)
                keep_c(cp * 2 + 1)
                norms(cp * 2 + 3, 1)
                deltas(cp * 2 + 1, 1)
                keep_c(cp * 2 + 2)
            deltas(CHUNKS - 2, 0)
            keep_c(CHUNKS - 1)
            deltas(CHUNKS - 1, 1)

            steps = [0]

            def link(ins):
                steps[0] += 1
                ins.then_inc(r_link, 1)
                dve.wait_ge(r_link, steps[0])

            def over_e(a):
                return a.unsqueeze(2).to_broadcast([P, TILES, E])

            def over_t(a):
                return a.unsqueeze(1).to_broadcast([P, TILES, E])

            dve.wait_ge(p1_act, CHUNKS * 3 + 3)
            for p in range(2):
                dve.wait_ge(du_out[p], CHUNKS * 16 + HEAD)
            link(dve.tensor_scalar(aff[:], aff[:], 1.0, None, ALU.add))
            link(dve.reciprocal(aff[:], aff[:]))
            src = aff[:]
            for j in range(TOPK):
                link(dve.tensor_reduce(top[:, j, :], src, AX, ALU.max))
                link(dve.tensor_tensor(eq, src, over_e(top[:, j, :]), ALU.is_equal))
                link(dve.scalar_tensor_tensor(cand, eq, float(-E), over_t(iota_sb[:, 0:E]), ALU.mult, ALU.add))
                link(dve.tensor_reduce(pick[:, j, :], cand, AX, ALU.min))
                link(dve.tensor_tensor(O[j], cand, over_e(pick[:, j, :]), ALU.is_equal))
                if j == 0:
                    link(dve.scalar_tensor_tensor(aff2, O[0], -4.0, aff[:], ALU.mult, ALU.add))
                    src = aff2
            link(dve.tensor_tensor(Osum, O[0], O[1], ALU.add))
            dve.sem_inc(picked, 1)
            link(dve.tensor_tensor(rsum[:], top[:, 0, :], top[:, 1, :], ALU.add))
            link(dve.reciprocal(rsum[:], rsum[:]))
            for j in range(TOPK):
                link(dve.tensor_tensor(top[:, j, :], top[:, j, :], rsum[:], ALU.mult))
            link(dve.tensor_tensor(eq, O[0], over_e(top[:, 0, :]), ALU.mult))
            link(dve.tensor_tensor(Wtmp, O[1], over_e(top[:, 1, :]), ALU.mult))
            link(dve.tensor_tensor(W[:, :, 0:E], eq, Wtmp, ALU.add))
            dve.wait_ge(rank_done, 2)
            link(dve.tensor_copy(cnt, hT[1][:].rearrange("p (t e) -> p e t", e=E)))
            flat = "p e t -> p (e t)"
            link(dve.tensor_tensor_scan(cum.rearrange(flat), mask_sb[:].rearrange(flat), cnt.rearrange(flat), 0.0,
                                        ALU.mult, ALU.add))
            link(dve.tensor_tensor(excl, cum, cnt, ALU.subtract))
            link(dve.tensor_scalar(per_e_u[:], cum[:, :, TILES - 1], float(P - 1), None, ALU.add))
            link(dve.tensor_scalar(per_e_u[:], per_e_u[:], 7, None, ALU.logical_shift_right))
            link(dve.tensor_copy(per_e[:, 0, :], per_e_u[:]))
            link(dve.tensor_tensor_scan(per_e[:, 1, :], per_e[:, 2, :], per_e[:, 0, :], 0.0, ALU.mult, ALU.add))
            link(dve.tensor_tensor(per_e[:, 3, :], per_e[:, 1, :], per_e[:, 0, :], ALU.subtract))
            link(dve.tensor_scalar(per_e[:, 3, :], per_e[:, 3, :], float(P), None, ALU.mult))
            link(dve.tensor_tensor(bcmp, bidx_sb[:], per_e[0:1, 1, :].unsqueeze(1).to_broadcast([1, BLOCKS, E]),
                                   ALU.is_ge))
            routed = be0_sb[:, 0:CHUNKS * (BPC + 1)].rearrange("o (c b) -> o c b", c=CHUNKS)[:, :, 0:BPC]
            link(dve.tensor_reduce(routed, bcmp.rearrange("o (c b) e -> o c b e", c=CHUNKS), AX, ALU.add))
            link(dve.tensor_scalar(routed, routed, float(E - 1), None, ALU.min))
            link(dve.tensor_copy(be_u[:], be0_sb[:]))
            dve.sem_inc(be_done, 1)
            link(dve.tensor_tensor(pos, hT[0][:].rearrange("p (t e) -> p t e", e=E), excl.rearrange("p e t -> p t e"),
                                   ALU.add))
            link(dve.tensor_tensor(pos, pos, over_t(per_e[:, 3, :]), ALU.add))
            for j in range(TOPK):
                link(dve.tensor_tensor(eq, O[j], pos, ALU.mult))
                link(dve.tensor_reduce(slot_f[:, j, :], eq, AX, ALU.add))
            link(dve.tensor_copy(slot_u[:], slot_f[:]))
            link(dve.tensor_scalar(part_u[:, 0], slot_u[:], P - 1, None, ALU.bitwise_and))
            link(dve.tensor_scalar(part_u[:, 1], slot_u[:], 7, None, ALU.logical_shift_right))
            link(dve.tensor_copy(part_f[:], part_u[:]))
            for j in range(TOPK):
                dve.tensor_tensor(rows[j], iota_sb[:].unsqueeze(1).to_broadcast([P, TILES, P]),
                                  part_f[:, 0, j, :].unsqueeze(2).to_broadcast([P, TILES, P]), ALU.is_equal)\
                    .then_inc(row_done, 1)
                for half in range(2):
                    for t in range(TILES // 2):
                        tile = half * (TILES // 2) + t
                        last = dve.tensor_scalar(cols_at[j][half][:, t, :], iota_sb[:, 0:BLOCKS + 1],
                                                 part_f[:, 1, j, tile:tile + 1], tokid_sb[:, tile:tile + 1],
                                                 ALU.is_equal, ALU.mult)
                    last.then_inc(col_done, 1)
            dve.wait_ge(tok_pe, 1)
            dve.tensor_copy(tok_sb[:], hT[2][:, 0:BLOCKS + 1]).then_inc(tok_done, 1)

            for p in range(2):
                dve.wait_ge(p1_out[p], CHUNKS // 2 * 16 + HEAD)
            dve.memset(state[:], 0.0)
            dve.memset(yacc[:], 0.0).then_inc(cleared, 1)
            dve.wait_ge(cleared, 1)

            def z_add(c, g):
                dve.wait_ge(yT_done, c * G + (g + 1 + HEAD))
                dve.scalar_tensor_tensor(zT[:, g, :], x0T[:, g, :], dpar[:, g:g + 1], FP[g % 2][:],
                                         ALU.mult, ALU.add).then_inc(z_done, 1)

            def step(c, n, k, kind=None, i=None, nxt=0, first=False):
                unit = (c + nxt) * UNITS + (0 if nxt else n) * G

                def scan(g):
                    if g == 0 and not first:
                        dve.wait_ge(state_done, (c + nxt) * NS + (0 if nxt else n) - 1 + HEAD)
                    dve.wait_ge(exp_done, unit + g + 1)
                    dve.wait_ge(dbx_done, unit + g + 1)
                    dve.tensor_tensor_scan(h[:, k % 2, g, :], dA[g % 2][:], dbx[:, g, :],
                                           state[:, g, bass.ds(begin_next if nxt else begin + n, 1)],
                                           ALU.mult, ALU.add).then_inc(scan_done, 1)

                def y_add(s):
                    if first:
                        return
                    count = c * (NS * YT) + (n - 1) * YT + s + 1
                    dve.wait_ge(hT_done, count)
                    dve.wait_ge(y_done, count - YT + HEAD)
                    if s == 0 and kind == "routed" and k == 1:
                        dve.wait_ge(yzero_done, c * YT + HEAD)
                    y = yacc[:, bass.ds(half + s, 1), :].rearrange("p o d -> p (o d)")
                    dve.scalar_tensor_tensor(y, hT[s][:], cc[:, bass.ds(c * TS + s, 1), bass.ds(n - 1, 1)], y,
                                             ALU.mult, ALU.add).then_inc(y_done, 1)

                def hidden(e, f):
                    dve.wait_ge(ffn_done, (c * SH + e) * FFN + FT + f + 2)
                    dve.wait_ge(gelu_done, (c * SH + e) * FT + f + 1)
                    dve.scalar_tensor_tensor(hid[:, f, :], FP[f][:], eb_sb[:, 1, e, f:f + 1], hg[:, f, :],
                                             ALU.add, ALU.mult).then_inc(hid_done, 1)

                def combine(e, s):
                    dve.wait_ge(ffn_done, (c * SH + e) * FFN + 2 * FT + s + 2)
                    dve.wait_ge(comb_done, (c * SH + e) * TS + s + 1 - TS + HEAD)
                    dve.tensor_tensor(facc[:, s, :], FP[s % 2][:], facc[:, s, :], ALU.add).then_inc(comb_done, 1)

                def seed(s):
                    if s == 0:
                        dve.wait_ge(f_out, c * 16 + 16 + HEAD)
                        dve.wait_ge(n_in, c * 16 + 16)
                    dve.wait_ge(bias_done, c * TS + s + 1)
                    dve.tensor_tensor(facc[:, s, :], FP[s % 2][:], xn0[:, s, :], ALU.add).then_inc(facc_done, 1)

                def extra(after):
                    at = (kind, k, after)
                    for do, what in EXTRAS.get(at, ()):
                        if do == "z":
                            z_add(c, *what)
                        elif do == "seed":
                            seed(*what)
                        elif do == "hidden":
                            hidden(*what)
                        else:
                            combine(*what)

                block = c * BPC + i if kind == "routed" else None
                scan(0)
                scan(1)
                y_add(0)
                extra(0)
                late = (kind, k) in (("shared0", 3), ("shared2", 1))
                if not late:
                    scan(2)
                y_add(1)
                extra(1)
                if late:
                    scan(2)
                scan(3)
                if kind == "routed" and k == 3:
                    dve.wait_ge(blk_act, block * 3 + 3)
                    dve.tensor_tensor(hidr[:], FP[1][:, F:2 * F], hgr[:], ALU.mult).then_inc(blk_dve, 1)
                y_add(2)
                extra(2)
                extra(3)
                if kind == "routed" and k == 0:
                    dve.wait_ge(yo_out, block * 16 + HEAD)
                    wait_alone(dve, blk_pe, block * 4 + 5)
                    dve.tensor_copy(yo[:], FP[1][:]).then_inc(blk_dve, 1)

            begin = NS
            step(0, 0, 0, first=True)
            with dve.Fori(0, CHUNKS) as c:
                begin = dve.value_load(ctab_sb[0:1, bass.ds(c, 1), 0], min_val=0, max_val=NS)
                begin_next = dve.value_load(ctab_sb[0:1, bass.ds(c + 1, 1), 0], min_val=0, max_val=NS)
                half = dve.value_load(ctab_sb[0:1, bass.ds(c, 1), 1], min_val=0, max_val=TS)
                with dve.Fori(0, BPC) as i:
                    for k in range(1, NPI + 1):
                        step(c, i * NPI + k, k % NPI, "routed", i)
                for i, kind in KINDS.items():
                    for k in range(1, NPI + 1):
                        step(c, i * NPI + k, k % NPI, kind, i, nxt=int(i * NPI + k == NS))
            for g in range(G):
                z_add(CHUNKS, g)

            with dve.Fori(0, CHUNKS // 2) as cp:
                for p in range(2):
                    c = cp * 2 + p
                    dve.wait_ge(in4[p], cp * 48 + 48)
                    dve.wait_ge(rows4[p], (cp + 1) * (TOPK * TS * 16))
                    for j in range(TOPK):
                        for s in range(TS):
                            last = dve.scalar_tensor_tensor(f4[p][:, s, :], r4[p][j][:, s, :],
                                                            top[:, j, bass.ds(c * TS + s, 1)], f4[p][:, s, :],
                                                            ALU.mult, ALU.add)
                        last.then_inc(f4_done, 1)
                        dve.wait_ge(f4_done, c * TOPK + j + 1)
                    dve.wait_ge(silu_done, c + 1)
                    dve.tensor_tensor(s4[p][:], s4[p][:], f4[p][:], ALU.mult).then_inc(g4_done, 1)
                    dve.wait_ge(g4_done, c + 1)
                    dve.tensor_tensor(x4[p][:], x4[p][:], s4[p][:], ALU.add).then_inc(o4_done, 1)

        @block.tensor
        def _(pe):
            pe.wait_ge(const_in, 16 * len(consts))
            pe.wait_ge(dve_const, 2)
            for done, n in ((p1_tr, 2 * G), (blk_pe, 1), (ffn_done, 1), (yT_done, HEAD), (yL_done, HEAD)):
                pe.sem_inc(done, n)

            def transposes(c, p):
                for r, (src, banks) in enumerate(((n_b[p], x_bank), (h_b[p], pre_bank))):
                    pe.wait_ge(p1_norm, c * 2 + r + 1)
                    if r == 0:
                        pe.wait_ge(p1_act, c * 3 + 3)
                        pe.wait_ge(cc_done, c + 1)
                    else:
                        pe.wait_ge(relu_done, c * G + G)
                    for g in range(G):
                        for s in range(TS):
                            last = pe.transpose(banks[g][:, s * P:(s + 1) * P], src[:, s, g * P:(g + 1) * P], eye_sb[:])
                        last.then_inc(p1_tr, 1)

            def projections(c, p):
                xnT = t_b[p]
                pe.wait_ge(p1_cp, c * (2 * G) + G)
                for s in range(TS):
                    for k in range(G):
                        last = pe.matmul(hT[3][:, s * E:(s + 1) * E], x0T[:, k, s * P:(s + 1) * P], wa_sb[:, k, :],
                                         start=(k == 0), stop=(k == G - 1))
                last.then_inc(p1_pe, 1)
                pe.wait_ge(p1_cp, c * (2 * G) + 2 * G)
                for bank, at in ((hT[0], 0), (hT[1], RANK)):
                    for k in range(G):
                        last = pe.matmul(bank[:], xpw_sb[:, k, at:at + P], xnT[:, k, :], start=(k == 0),
                                         stop=(k == G - 1))
                    last.then_inc(p1_pe, 1)
                pe.wait_ge(p1_act, c * 3 + 5)
                for g in range(G):
                    pe.matmul(pre_bank[g][:], dtw_sb[:, g * P:(g + 1) * P], drT[:], start=True, stop=True)\
                        .then_inc(pre_done, 1)
                pe.wait_ge(p1_act, c * 3 + 6)
                for s in range(TS):
                    last = pe.transpose(hT[3][:, s * P:(s + 1) * P], bcT[:, s * P:(s + 1) * P], eye_sb[:])
                last.then_inc(p1_pe, 1)

            transposes(0, 0)
            with pe.Fori(0, CHUNKS // 2 - 1) as cp:
                projections(cp * 2, 0)
                transposes(cp * 2 + 1, 1)
                projections(cp * 2 + 1, 1)
                transposes(cp * 2 + 2, 0)
            projections(CHUNKS - 2, 0)
            transposes(CHUNKS - 1, 1)
            projections(CHUNKS - 1, 1)

            pe.wait_ge(picked, 1)
            pe.wait_ge(p1_act, CHUNKS * 3 + 3)
            pe.wait_ge(cc_done, CHUNKS + 1)
            for w, bank in ((tri_sb, hT[0]), (ones_sb, hT[1])):
                pe.matmul(bank[:], w[:], Osum.rearrange("p t e -> p (t e)"), start=True, stop=True)\
                    .then_inc(rank_done, 1)
            for j in range(TOPK):
                pe.wait_ge(row_done, j + 1)
                for half in range(2):
                    pe.wait_ge(col_done, j * 2 + half + 1)
                    for t in range(TILES // 2):
                        tile = half * (TILES // 2) + t
                        last = pe.matmul(hT[2][:, 0:BLOCKS + 1], rows[j][:, tile, :], cols_at[j][half][:, t, :],
                                         start=(j + tile == 0), stop=(j * TILES + tile == TOPK * TILES - 1))
            last.then_inc(tok_pe, 1)
            pe.wait_ge(cleared, 1)

            def clear_y():
                pe.matmul(y_bank[:], eye_sb[:], zero[:], start=True, stop=False).then_inc(y_clear, 1)

            clear_y()

            def y_part(c, g, blocks):
                if g == 0:
                    pe.wait_ge(ycopy_done, c * TS + YT)
                if g < 2:
                    pe.wait_ge(blk_act, blocks * 3 + 1)
                    pe.wait_ge(blk_dve, blocks * 2 + 1)
                    pe.wait_ge(comb_done, c * (SH * TS) + HEAD)
                else:
                    pe.wait_ge(z_done, c * G + g - 1 + HEAD)
                for s in range(TS):
                    last = pe.transpose(FP[g % 2][:, s * P:(s + 1) * P], yprev[:, s, g * P:(g + 1) * P], eye_sb[:])
                last.then_inc(yT_done, 1)

            def s_part(c, s, k):
                if k == 0:
                    if s == 0:
                        pe.wait_ge(z_done, c * G + G + HEAD)
                    pe.wait_ge(sc_done, c * TS + max(s - 1, 0) + HEAD)
                last = pe.matmul(FP[s % 2][:], zT[:, k, s * P:(s + 1) * P], ow_sb[:, k, :],
                                 start=(k == 0), stop=(k == G - 1))
                if k == G - 1:
                    last.then_inc(s_done, 1)

            with pe.Fori(0, CHUNKS) as c:

                def x_part(g):
                    if g == "w":
                        pe.wait_ge(wc_done, c + 1)
                        pe.wait_ge(xTc_done, c * G + G)
                        for s in range(TS):
                            last = pe.transpose(FP[0][0:ITEMS, s * P:(s + 1) * P], Wc[:, s, :], eye_sb[:])
                        last.then_inc(wt_done, 1)
                        return
                    if g == 0:
                        pe.wait_ge(n_in, c * 16 + 16)
                    if g < 2:
                        pe.wait_ge(sc_done, c * TS + TS - 1 + g + HEAD)
                    else:
                        pe.wait_ge(xTc_done, c * G + g - 1)
                    for s in range(TS):
                        last = pe.transpose(FP[g % 2][:, s * P:(s + 1) * P], xn0[:, s, g * P:(g + 1) * P], eye_sb[:])
                    last.then_inc(xT_done, 1)

                def bias_part(s):
                    if s == 0:
                        pe.wait_ge(wtc_done, c + 1)
                    if s >= 2:
                        pe.wait_ge(facc_done, c * TS + s - 1 + HEAD)
                    pe.matmul(FP[s % 2][:], WT[:, s * P:(s + 1) * P], eb2_sb[:], start=True, stop=True)\
                        .then_inc(bias_done, 1)

                def shared_part(e, kind, j, q):
                    expert = c * SH + e
                    bank = FP[j % 2]
                    use = c * USES + BPC + e
                    if kind == "down":
                        if (j, q) == (0, 0):
                            pe.wait_ge(wd_in, use * 16 + 16)
                            pe.wait_ge(hid_done, expert * FT + FT)
                        elif j >= 2 and q == 0:
                            pe.wait_ge(comb_done, expert * TS + (j - 1) + HEAD)
                        last = pe.matmul(bank[:], hid[:, q, j * P:(j + 1) * P], wd[:, q, :],
                                         start=(q == 0), stop=(q == FT - 1))
                        if q == FT - 1:
                            last.then_inc(ffn_done, 1)
                        return
                    if kind == "gate" and q == 0:
                        if j == 0:
                            pe.wait_ge(gu_in, use * 32 + 32)
                        pe.wait_ge(comb_done, expert * TS - FT + j + 1 + HEAD)
                        pe.wait_ge(facc_done, c * TS + TS + HEAD)
                    if kind == "up" and q == 0:
                        pe.wait_ge(gelu_done, expert * FT + j + 1)
                    gu = 0 if kind == "gate" else 1
                    last = pe.matmul(bank[:], wgu[:, q, gu, j * P:(j + 1) * P], x0T[:, q, :],
                                     start=(q == 0), stop=(q == G - 1))
                    if q == G - 1:
                        last.then_inc(ffn_done, 1)

                def block_part(i, what):
                    v = c * BPC + i
                    use = c * USES + i
                    if what == "tokens":
                        pe.wait_ge(xg_in, v * 16 + 16)
                        pe.wait_ge(blk_act, v * 3 + 1)
                        pe.wait_ge(comb_done, c * (SH * TS) + HEAD)
                        for k in range(G):
                            last = pe.transpose(FP[0][:, k * P:(k + 1) * P], xg[:, k * P:(k + 1) * P], eye_sb[:])
                        last.then_inc(blk_pe, 1)
                    elif what == "biases":
                        pe.wait_ge(gu_in, use * 32 + 32)
                        pe.wait_ge(blk_dve, v * 2 + 1)
                        pe.matmul(FP[1][:], ones_sb[0:1, :], brow[0:1, :], start=True, stop=False)
                    elif type(what) is int:
                        if what == 0:
                            pe.wait_ge(blk_act, v * 3 + 2)
                        last = pe.matmul(FP[1][:], xgT[:, what, :], wgu[:, what, :, :].rearrange("p g f -> p (g f)"),
                                         start=False, stop=(what == G - 1))
                        if what == G - 1:
                            last.then_inc(blk_pe, 1)
                    elif what == "hidden":
                        pe.wait_ge(blk_dve, v * 2 + 2)
                        for f in range(FT):
                            last = pe.transpose(FP[0][:, f * P:(f + 1) * P], hidr[:, f * P:(f + 1) * P], eye_sb[:])
                        last.then_inc(blk_pe, 1)
                    else:
                        f = int(what[-1])
                        if f == 0:
                            pe.wait_ge(wd_in, use * 16 + 16)
                            pe.wait_ge(blk_act, v * 3 + 4)
                        last = pe.matmul(FP[1][:], hidrT[:, f, :], wd[:, f, :], start=(f == 0), stop=(f == FT - 1))
                        if f == FT - 1:
                            last.then_inc(blk_pe, 1)

                def body(i, kind=None):
                    for k in range(NPI):
                        pe.wait_ge(scan_done, c * UNITS + i * (NPI * G) + (k * G + G + HEAD))

                        def transpose(bank, s):
                            for g in range(G):
                                last = pe.transpose(bank[:, g * P:(g + 1) * P], h[:, k % 2, g, s * P:(s + 1) * P],
                                                    eye_sb[:])
                            return last

                        pe.wait_ge(y_done, c * (NS * YT) + i * (NPI * YT) + (k * YT + HEAD))
                        transpose(hT[YT - 1], YT).then_inc(hL_done, 1)
                        early = kind == "shared2" and k == NPI - 1
                        for s in range(TS):
                            if s < YT - 1:
                                pe.wait_ge(y_done, c * (NS * YT) + i * (NPI * YT) + (k * YT + s + 1 - YT + HEAD))
                                transpose(hT[s], s).then_inc(hT_done, 1)
                            elif s == YT - 1:
                                pe.wait_ge(ch_done, c * NS + i * NPI + (k + 1))
                                transpose(hT[s], s).then_inc(hT_done, 1)
                            if s == (1 if early else TS - 1):
                                pe.wait_ge(ch_done, c * NS + i * NPI + (k + 1))
                                pe.matmul(y_bank[:], eye_sb[:], ch[:], start=False, stop=early).then_inc(yL_done, 1)
                            for part in SLOTS[kind].get(k * TS + s, ()):
                                if kind == "routed":
                                    block_part(i, part)
                                elif kind.startswith("shared"):
                                    shared_part(part[0], *part[1])
                                elif type(part) is tuple:
                                    s_part(c, *part)
                                elif kind == "y":
                                    y_part(c, part, (c + 1) * BPC)
                                elif type(part) is int:
                                    bias_part(part)
                                else:
                                    x_part(int(part[1]) if part != "w" else "w")

                with pe.Fori(0, BPC) as i:
                    body(i, "routed")
                for i, kind in KINDS.items():
                    body(i, kind)
                pe.wait_ge(ycopy_done, c * TS + TS)
                clear_y()
            for g in range(G):
                y_part(CHUNKS, g, BLOCKS)
            for s in range(TS):
                for k in range(G):
                    s_part(CHUNKS, s, k)


def kernel(**inputs):
    import numpy as np
    import concourse.bacc as bacc
    from concourse.bass_utils import run_bass_kernel_spmd

    v = {k.removeprefix("L0_"): np.asarray(a) for k, a in inputs.items()}

    def tiles(a):
        return a.reshape(-1, P, *a.shape[1:]).swapaxes(0, 1)

    def both(r, s):
        return np.concatenate([v["ffn_" + r], v["ffn_" + s]], 0)

    def by_k(w):
        return w.reshape(ITEMS, -1, P, w.shape[2]).swapaxes(1, 2)

    gate_up = np.stack([by_k(both("rg", "sg")), by_k(both("rw1", "sw1"))], 3).reshape(ITEMS, P, -1)
    down = by_k(both("rw2", "sw2")).reshape(ITEMS, P, -1)
    use_expert = np.zeros((1, CHUNKS * (BPC + 1) + 1), np.float32)
    use_expert[0, BPC:-1:BPC + 1] = E
    mask = np.ones((P, E, TILES), np.float32)
    mask[:, :, 0] = 0
    arrays = {
        "x": v["attn_x"].reshape(-1, DIM),
        "xpw": tiles(v["attn_x_proj_w"].T),
        "dtw": v["attn_dt_proj_w"].T,
        "wa": tiles(v["ffn_wa"]),
        "ow": tiles(v["attn_out_proj_w"].T),
        "cols": np.stack([v["attn_norm_w"], v["attn_norm_b"], v["attn_dt_proj_b"], v["attn_D_param"]])
        .reshape(4, G, P).transpose(2, 0, 1),
        "a_log": tiles(v["attn_A_log"]),
        "ew": np.concatenate([gate_up, down], 2),
        "eb": np.stack([v["ffn_sgb"], v["ffn_sb1"]]).reshape(2, SH, FT, P).transpose(3, 0, 1, 2),
        "ebr": np.concatenate([both("rgb", "sgb"), both("rb1", "sb1")], 1),
        "eb2": both("rb2", "sb2"),
        "eye": np.eye(P, dtype=np.float32),
        "tri": np.triu(np.ones((P, P), np.float32), 1),
        "iota": np.tile(np.arange(P, dtype=np.float32), (P, 1)),
        "mask": mask,
        "bidx": np.repeat(np.arange(BLOCKS, dtype=np.float32), E).reshape(1, BLOCKS, E),
        "be0": use_expert,
        "ctab": np.array([[NS * (c % CPB == 0), TS * (c % 2), TS * ((c + 1) % 2)] for c in range(CHUNKS + 1)],
                         np.uint32)[None],
        "tokid": np.arange(BATCH * SEQ, dtype=np.float32).reshape(TILES, P).T,
    }
    arrays = {"in_" + k: np.ascontiguousarray(a) for k, a in arrays.items()}
    nc = bacc.Bacc("TRN2", target_bir_lowering=False, num_devices=1)
    args = [nc.dram_tensor(k, a.shape, mybir.dt.from_np(a.dtype), kind="ExternalInput").ap() for k, a in arrays.items()]
    args.append(nc.dram_tensor("out", [BATCH * SEQ, DIM], F32, kind="ExternalOutput").ap())
    build(nc, *args)
    r = run_bass_kernel_spmd(nc, [arrays], core_ids=[0])
    return r.results[0]["out"].reshape(BATCH, SEQ, DIM)
```
